# Optimizing a Trainium2 kernel written in Bass

```python
import numpy as np
import jax
import jax.numpy as jnp

def _softmax(x, axis=-1):
    return jax.nn.softmax(x, axis=axis)

def _gelu(x):
    return jax.nn.gelu(x, approximate=True)

def _silu(x):
    return jax.nn.silu(x)

def _sigmoid(x):
    return jax.nn.sigmoid(x)

def _layernorm(x, axis=-1, eps=1e-05):
    m = jnp.mean(x, axis=axis, keepdims=True)
    v = jnp.var(x, axis=axis, keepdims=True)
    return (x - m) / jnp.sqrt(v + eps)

def _scatter_add(tgt, idx, src, axis=0):
    return tgt.at[idx].add(src)

def _segment_sum(src, seg, n):
    return jax.ops.segment_sum(src, seg, n)
kernel_name = 'mk_gnn_preln_d1_gnn_r32_a0715b'

def setup_inputs(seed: int=0):
    np.random.seed(seed)
    _w = jnp.asarray

    def _rec_inputs():
        import jax
        import jax.numpy as jnp
        _gk = jax.random.key(seed)
        x = -0.0009044 + 1 * jax.random.normal(jax.random.fold_in(_gk, 1), (3125, 16), jnp.float32)
        _s = jax.random.randint(jax.random.fold_in(_gk, 2), (50000,), 0, 3125, jnp.int32)
        _d = jax.random.randint(jax.random.fold_in(_gk, 3), (50000,), 0, 3125, jnp.int32)
        _loop = jnp.arange(3125, dtype=jnp.int32)
        src = jnp.concatenate([_s, _d, _loop])
        dst = jnp.concatenate([_d, _s, _loop])
        _o = jnp.argsort(dst, stable=True)
        src = src[_o]
        dst = dst[_o]
        edge_attr_64 = -2.32664e-05 + 0.999985 * jax.random.normal(jax.random.fold_in(_gk, 12), (103125, 64), jnp.float32)
        edge_weight1 = jax.random.uniform(jax.random.fold_in(_gk, 13), (103125, 1), jnp.float32, 0.0, 1)
        return (x, src, dst, edge_attr_64, edge_weight1)
    x, src, dst, edge_attr_64, edge_weight1 = _rec_inputs()

    def _L0_gnn_setup():
        import jax, jax.numpy as jnp
        import numpy as np
        N_NODES = 3125
        N_EDGES = 200000
        H = 16
        RF_DIM = 64
        key = jax.random.key(seed)
        ks = jax.random.split(key, 7)
        feat = jax.random.normal(ks[0], (N_NODES, H), dtype=jnp.float32)
        review_feat = jax.random.normal(ks[1], (N_EDGES, RF_DIM), dtype=jnp.float32)
        edge_w = jax.random.uniform(ks[2], (N_EDGES, 1), dtype=jnp.float32)
        src_idx = jax.random.randint(ks[3], (N_EDGES,), 0, N_NODES, dtype=jnp.int32)
        dst_idx = jax.random.randint(ks[4], (N_EDGES,), 0, N_NODES, dtype=jnp.int32)
        b1 = float(np.sqrt(6.0 / (H + H)))
        W_node = jax.random.uniform(ks[5], (H, H), minval=-b1, maxval=b1, dtype=jnp.float32)
        b2 = float(np.sqrt(6.0 / (H + RF_DIM)))
        W_review = jax.random.uniform(ks[6], (H, RF_DIM), minval=-b2, maxval=b2, dtype=jnp.float32)
        return {'feat': feat, 'review_feat': review_feat, 'edge_w': edge_w, 'src_idx': src_idx, 'dst_idx': dst_idx, 'W_node': W_node, 'W_review': W_review}
    _L0_gnn_all = _L0_gnn_setup()
    _L0_gnn_in = {k: v for k, v in _L0_gnn_all.items() if k in ('W_node', 'W_review')}
    del _L0_gnn_all
    return {'x': x, 'src': src, 'dst': dst, 'edge_attr_64': edge_attr_64, 'edge_weight1': edge_weight1, 'L0_gnn_W_node': _L0_gnn_in['W_node'], 'L0_gnn_W_review': _L0_gnn_in['W_review']}

def reference(x, src, dst, edge_attr_64, edge_weight1, L0_gnn_W_node, L0_gnn_W_review):
    import jax
    import jax.numpy as jnp

    def _L0_gnn_ref(feat, review_feat, edge_w, src_idx, dst_idx, W_node, W_review):
        import jax, jax.numpy as jnp
        import numpy as np
        N_NODES = 3125
        N_EDGES = 200000
        H = 16
        RF_DIM = 64
        h = feat @ W_node.T
        rf = review_feat @ W_review.T
        m = (h[src_idx] + rf) * edge_w
        rst = jax.ops.segment_sum(m, dst_idx, num_segments=N_NODES)
        return rst
    h = jnp.maximum(_layernorm(x, axis=-1), 0.0)
    x = x + _L0_gnn_ref(h, edge_attr_64, edge_weight1, src, dst, L0_gnn_W_node, L0_gnn_W_review)
    return x

_drawn_inputs = setup_inputs


def setup_inputs(seed=0):
    import zlib

    import numpy as np

    out = dict(_drawn_inputs(seed))
    spreads = {}
    factors = {}
    for name, (base, spread) in spreads.items():
        noise = np.random.default_rng([zlib.crc32(name.encode()), seed]).standard_normal(out[name].shape)
        drawn = base * np.exp(spread * noise) if base else spread * noise
        out[name] = jnp.asarray(drawn.astype(out[name].dtype))
    for name, factor in factors.items():
        out[name] = (out[name] * factor).astype(out[name].dtype)
    return out
```

```python
import concourse.bass as bass
from concourse import mybir
from contextlib import ExitStack

F32, F16, I32 = mybir.dt.float32, mybir.dt.float16, mybir.dt.int32
ALU = mybir.AluOpType
ACT = mybir.ActivationFunctionType
AX = mybir.AxisListType

P = 128
H = 16
F = 64
HALVES, GRP = 2, 4
TILES = HALVES * GRP
HALF = GRP * P
SC = HALVES * HALF
WIN = 64
BLK = 4
PARTS = 7
LO_ROWS = 112
SCALE = 4096.0
MASK = -16384.0
EPS = 1e-5
MATMUL, ROWS = "matmul", "rows"
KINDS = [MATMUL, ROWS, MATMUL, MATMUL, ROWS, MATMUL]
SETS = 2
PER = len(KINDS) // SETS
BANK = 512


def gnn_kernel(nc, x, src, dst, attr, weight, w_node, w_review, out):
    N, E = x.shape[0], attr.shape[0]
    NS = -(-E // SC)
    OVER = NS * SC - E
    STEP = SC * N // E
    HSTEP = (STEP + 1) // 2
    LEAD = (WIN - HSTEP) // 2 - 1
    FULL = NS // len(KINDS)
    REST = KINDS[:NS - FULL * len(KINDS)]
    COLS = max((NS - 1) * STEP + HSTEP + WIN, LEAD + N)
    NODES_P = BLK * PARTS
    XP = N // NODES_P
    XR = N - XP * NODES_P
    OG = 25
    OP = N // OG
    BLOCKS = -(-N // BANK)
    assert OG * OP == N and XP < LO_ROWS and LO_ROWS * NODES_P >= N

    lo_dram = nc.dram_tensor("lo_dram", (NS, SC), F16, kind="Internal").ap()
    b_dram = nc.dram_tensor("b_dram", (NS, SC), F16, kind="Internal").ap()
    h_dram = nc.dram_tensor("h_dram", (N, H), F32, kind="Internal").ap()

    mm_slots = [j for j, kind in enumerate(KINDS) if kind == MATMUL]
    row_slots = [j for j, kind in enumerate(KINDS) if kind == ROWS]

    with ExitStack() as ctx:
        def sb(name, shape, dt):
            return ctx.enter_context(nc.sbuf_tensor(name, shape, dt))

        def pb(name, shape):
            return ctx.enter_context(nc.psum_tensor(name, shape, F32))

        def sem(name):
            return ctx.enter_context(nc.semaphore(name))

        ident = sb("ident", [P, P], F32)
        iota = sb("iota", [P, BANK], F32)
        base = sb("base", [P, NS, TILES], F32)
        lo_id = sb("lo_id", [P, PARTS], F32)
        ones = sb("ones", [P, 1], F32)
        src_row = sb("src_row", [NS, SC], I32)
        dst_row = sb("dst_row", [NS, SC], I32)
        w_row = sb("w_row", [NS, SC], F32)
        srcf_row = sb("srcf_row", [NS, SC], F32)
        dstf_row = sb("dstf_row", [NS, SC], F32)
        lo_int = sb("lo_int", [NS, SC], I32)
        b_int = sb("b_int", [NS, SC], I32)
        lo16 = sb("lo16", [NS, SC], F16)
        b16 = sb("b16", [NS, SC], F16)
        dst_w = sb("dst_w", [P, NS, 2, TILES], F32)
        src_t = sb("src_t", [P, NS, TILES], I32)
        xs = sb("xs", [P, NODES_P, H], F32)
        xc = sb("xc", [P, NODES_P, H], F32)
        sq = sb("sq", [P, NODES_P, H], F32)
        hn = sb("hn", [P, NODES_P, H], F32)
        hs = sb("hs", [P, NODES_P, H], F32)
        stat = sb("stat", [P, 5, NODES_P], F32)
        h_hi = sb("h_hi", [P, PARTS, BLK * H], F16)
        h_lo = sb("h_lo", [P, PARTS, BLK * H], F16)
        x_out = sb("x_out", [OP, OG * H], F32)
        w_cat = sb("w_cat", [H, P], F32)
        w_cat_t = sb("w_cat_t", [P, H], F32)
        V = sb("V", [P, len(KINDS), TILES, 2, F], F32)
        S = sb("S", [P, len(KINDS), TILES, WIN], F32)
        lo_bc = sb("lo_bc", [P, len(mm_slots), SC], F16)
        one_hot = sb("one_hot", [P, 2, PARTS, SC], F16)
        dst_w_now = sb("dst_w_now", [P, SETS, PER, 2, TILES], F32)
        src_now = sb("src_now", [P, len(row_slots), TILES], I32)
        agg = sb("agg", [P, COLS], F32)
        reach = sb("reach", [P, 4], F32)
        outside = sb("outside", [1, 1], I32)
        out_sb = sb("out_sb", [OP, OG * H], F32)
        S_gen = sb("S_gen", [P, TILES, BANK], F32)
        dst_gen = sb("dst_gen", [P, BLOCKS + 1, TILES], F32)

        picked = [pb(f"picked{q}", [P, TILES, BLK * H]) for q in range(len(mm_slots))]
        acc = [pb(f"acc{u}", [P, BANK]) for u in range(SETS)]
        turned = [pb(f"turned{c}", [P, GRP, P]) for c in range(HALVES)]

        x_loaded, w_loaded = sem("x_loaded"), sem("w_loaded")
        src_loaded, dst_loaded, weight_loaded = sem("src_loaded"), sem("dst_loaded"), sem("weight_loaded")
        x_zeroed, constants = sem("x_zeroed"), sem("constants")
        fills_done, bits_ready = sem("fills_done"), sem("bits_ready")
        std_ready, var_ready = sem("std_ready"), sem("var_ready")
        h_ready, h_stored, parts_ready = sem("h_ready"), sem("h_stored"), sem("parts_ready")
        lo_ready, lo_stored = sem("lo_ready"), sem("lo_stored")
        floats_ready, turns_done, turns_read = sem("floats_ready"), sem("turns_done"), sem("turns_read")
        tables_ready, rings_zeroed = sem("tables_ready"), sem("rings_zeroed")
        reach_ready, reach_summed, flag_ready = sem("reach_ready"), sem("reach_summed"), sem("flag_ready")
        wcat_turned, wcat_ready = sem("wcat_turned"), sem("wcat_ready")

        attr_loaded = [sem(f"attr_loaded{j}") for j in range(len(KINDS))]
        S_ready = [sem(f"S_ready{j}") for j in range(len(KINDS))]
        scattered = [sem(f"scattered{j}") for j in range(len(KINDS))]
        lo_loaded = [sem(f"lo_loaded{q}") for q in range(len(mm_slots))]
        onehot_ready = [sem(f"onehot_ready{q}") for q in range(len(mm_slots))]
        picked_ready = [sem(f"picked_ready{q}") for q in range(len(mm_slots))]
        relu_done = [sem(f"relu_done{q}") for q in range(len(mm_slots))]
        dstw_staged = [sem(f"dstw_staged{u}") for u in range(SETS)]
        src_staged = [sem(f"src_staged{r}") for r in range(len(row_slots))]
        rows_fetched = [sem(f"rows_fetched{r}") for r in range(len(row_slots))]
        acc_added = [sem(f"acc_added{u}") for u in range(SETS)]
        dve_step, fetches_begun = sem("dve_step"), sem("fetches_begun")

        gen_step, gen_attr, gen_src, gen_rows = sem("gen_step"), sem("gen_attr"), sem("gen_src"), sem("gen_rows")
        gen_dst, gen_S, gen_acc, gen_added = sem("gen_dst"), sem("gen_S"), sem("gen_acc"), sem("gen_added")
        projected, out_ready, out_stored = sem("projected"), sem("out_ready"), sem("out_stored")

        def wait(eng, s, value):
            if not isinstance(value, int) or value > 0:
                eng.wait_ge(s, value)

        def rounds(eng, body):
            body(0, KINDS)
            with eng.Fori(1, FULL) as i:
                body(i, KINDS)
            body(FULL, REST)

        def edge_start(s):
            if isinstance(s, int):
                return min(s * SC, E - SC)
            return s * SC

        def superchunks(eng, body):
            with eng.Fori(0, NS - 1) as s:
                body(s, s * SC)
            body(NS - 1, E - SC)

        def load_rows(eng, row, flat, done):
            whole = flat[0:(NS - 1) * SC].rearrange("(s e) -> s e", e=SC)
            cut = (NS - 1) // 16 * 16
            eng.dma_start(row[0:cut, :], whole[0:cut, :]).then_inc(done, 16)
            eng.dma_start(row[cut:NS - 1, :], whole[cut:NS - 1, :]).then_inc(done, 16)
            eng.dma_start(row[NS - 1:NS, :], flat[E - SC:E].rearrange("(s e) -> s e", e=SC)).then_inc(done, 16)

        def load_attr(eng, j, first, done):
            for c in range(HALVES):
                eng.dma_start(V[:, j, c * GRP:(c + 1) * GRP, 0, :],
                              attr[bass.ds(first + c * HALF, HALF), :].rearrange("(p g) f -> p g f", g=GRP)
                              ).then_inc(done, 16)

        block = ctx.enter_context(nc.Block())

        @block.sync
        def _(sp):
            load_rows(sp, src_row, src, src_loaded)
            sp.dma_start(x_out[:, :], x.rearrange("(p j) d -> p (j d)", j=OG)).then_inc(w_loaded, 16)
            sp.dma_start(w_cat[:, 0:F], w_review).then_inc(w_loaded, 16)
            for b in range(BLK):
                sp.dma_start(w_cat[:, F + b * H:F + (b + 1) * H], w_node).then_inc(w_loaded, 16)
            sp.wait_ge(lo_ready, 2)
            sp.dma_start(lo_dram, lo16[:, :]).then_inc(lo_stored, 16)
            sp.dma_start(b_dram, b16[:, :]).then_inc(lo_stored, 16)

            def prefetch(i, kinds):
                for j, kind in enumerate(kinds):
                    s = i * len(KINDS) + j
                    u, q, r = j // PER, kinds[:j].count(MATMUL), kinds[:j].count(ROWS)
                    if j % PER == 0:
                        if isinstance(i, int) and i == 0 and j == 0:
                            sp.wait_ge(tables_ready, 1)
                        n = min(PER, len(kinds) - j)
                        wait(sp, S_ready[(u + 1) * PER - 1], i)
                        sp.dma_start(dst_w_now[:, u, 0:n, :, :].rearrange("p s k t -> p (s k t)"),
                                     dst_w[:, bass.ds(s, n), :, :].rearrange("p s k t -> p (s k t)")
                                     ).then_inc(dstw_staged[u], 16)
                    if kind == ROWS:
                        wait(sp, rows_fetched[r], i * (16 * TILES))
                        sp.dma_start(src_now[:, r, :], src_t[:, bass.ds(s, 1), :].rearrange("p s t -> p (s t)")
                                     ).then_inc(src_staged[r], 16)
                    else:
                        if isinstance(i, int) and i == 0 and j == 0:
                            sp.wait_ge(lo_stored, 32)
                        wait(sp, onehot_ready[q], i)
                        sp.dma_start(lo_bc[0:LO_ROWS, q, :],
                                     lo_dram[bass.ds(s, 1), :].to_broadcast([LO_ROWS, SC])
                                     ).then_inc(lo_loaded[q], 16)
                        sp.dma_start(lo_bc[LO_ROWS:P, q, :],
                                     b_dram[bass.ds(s, 1), :].to_broadcast([P - LO_ROWS, SC])
                                     ).then_inc(lo_loaded[q], 16)
                    wait(sp, scattered[j], i)
                    load_attr(sp, j, edge_start(s), attr_loaded[j])

            rounds(sp, prefetch)

            sp.wait_ge(flag_ready, 1)
            with sp.If(sp.value_load(outside[0:1, 0:1], min_val=0, max_val=P) > 0):
                def load_again(s, start):
                    sp.wait_ge(gen_added, s * BLOCKS + 1)
                    load_attr(sp, 1, start, gen_attr)
                    sp.dma_start(src_now[:, 0, :], src_t[:, bass.ds(s, 1), :].rearrange("p s t -> p (s t)")
                                 ).then_inc(gen_src, 16)
                    sp.dma_start(dst_w_now[:, 0, 0, :, :].rearrange("p k t -> p (k t)"),
                                 dst_w[:, bass.ds(s, 1), :, :].rearrange("p s k t -> p (s k t)")
                                 ).then_inc(gen_dst, 16)

                superchunks(sp, load_again)

            sp.wait_ge(out_ready, 1)
            sp.dma_start(out.rearrange("(p j) d -> p (j d)", j=OG), out_sb[:, :]).then_inc(out_stored, 16)
            sp.wait_ge(out_stored, 16)

        @block.gpsimd
        def _(pool):
            nc.gpsimd.memset(xs[:, :, :], 0.0).then_inc(x_zeroed, 1)
            nc.gpsimd.iota(lo_id[:, :], [[1, PARTS]], base=0, channel_multiplier=PARTS,
                           allow_small_or_imprecise_dtypes=True).then_inc(constants, 1)
            nc.gpsimd.memset(ident[:, :], 1.0).then_inc(fills_done, 1)
            nc.gpsimd.memset(h_hi[:, 1:PARTS, :], 0.0).then_inc(fills_done, 1)
            pool.wait_ge(fills_done, 2)
            nc.gpsimd.memset(h_hi[:, 0, :], MASK).then_inc(fills_done, 1)
            nc.gpsimd.affine_select(out=ident[:, :], in_=ident[:, :], compare_op=ALU.is_equal, fill=0.0, base=0,
                                    pattern=[[-1, P]], channel_multiplier=1).then_inc(constants, 1)
            pool.wait_ge(fills_done, 3)
            masks = h_hi[:, 0, :].rearrange("p (b d) -> p b d", b=BLK)
            nc.gpsimd.affine_select(out=masks, in_=masks, compare_op=ALU.not_equal, fill=0.0, base=-LO_ROWS,
                                    pattern=[[-1, BLK], [0, H]], channel_multiplier=1).then_inc(constants, 1)
            nc.gpsimd.memset(h_lo[:, :, :], 0.0).then_inc(constants, 1)
            nc.gpsimd.iota(iota[:, :], [[1, BANK]], base=0, channel_multiplier=0,
                           allow_small_or_imprecise_dtypes=True).then_inc(constants, 1)
            nc.gpsimd.iota(base[:, :, :], [[STEP, NS], [HSTEP, HALVES], [0, GRP]], base=-LEAD, channel_multiplier=0,
                           allow_small_or_imprecise_dtypes=True).then_inc(constants, 1)
            nc.gpsimd.memset(ones[:, :], 1.0).then_inc(constants, 1)
            for j in row_slots:
                nc.gpsimd.memset(V[:, j, :, 1, H:F], 0.0).then_inc(rings_zeroed, 1)

            def fetch_rows(i, kinds):
                for j, kind in enumerate(kinds):
                    if kind == ROWS:
                        r = kinds[:j].count(ROWS)
                        wait(pool, scattered[j], i)
                        pool.wait_ge(src_staged[r], (i + 1) * 16)
                        pool.sem_inc(fetches_begun, 1)
                        for t in range(TILES):
                            pool.indirect_dma_start(V[:, j, t, 1, 0:H], None, h_dram,
                                                    bass.IndirectOffsetOnAxis(src_now[:, r, t:t + 1], 0)
                                                    ).then_inc(rows_fetched[r], 16)

            pool.wait_ge(h_stored, 32)
            rounds(pool, fetch_rows)

            pool.wait_ge(flag_ready, 1)
            with pool.If(pool.value_load(outside[0:1, 0:1], min_val=0, max_val=P) > 0):
                def fetch_again(s, start):
                    pool.wait_ge(gen_added, s * BLOCKS + 1)
                    pool.wait_ge(gen_src, (s + 1) * 16)
                    pool.sem_inc(fetches_begun, 1)
                    for t in range(TILES):
                        pool.indirect_dma_start(V[:, 1, t, 1, 0:H], None, h_dram,
                                                bass.IndirectOffsetOnAxis(src_now[:, 0, t:t + 1], 0)
                                                ).then_inc(gen_rows, 16)

                superchunks(pool, fetch_again)

        @block.scalar
        def _(act):
            act.wait_ge(x_zeroed, 1)
            act.dma_start(xs[0:XP, :, :].rearrange("p n d -> p (n d)"),
                          x[0:XP * NODES_P, :].rearrange("(p n) d -> p (n d)", n=NODES_P)).then_inc(x_loaded, 16)
            act.dma_start(xs[XP:XP + 1, 0:XR, :].rearrange("p n d -> p (n d)"),
                          x[XP * NODES_P:N, :].rearrange("(p n) d -> p (n d)", n=XR)).then_inc(x_loaded, 16)
            load_rows(act, dst_row, dst, dst_loaded)
            load_rows(act, w_row, weight.rearrange("e one -> (e one)"), weight_loaded)
            act.wait_ge(src_loaded, 48)
            nc.scalar.activation(srcf_row[:, :], src_row[:, :], ACT.Copy).then_inc(floats_ready, 1)
            act.wait_ge(dst_loaded, 48)
            nc.scalar.activation(dstf_row[:, :], dst_row[:, :], ACT.Copy).then_inc(floats_ready, 1)
            act.wait_ge(var_ready, 1)
            nc.scalar.activation(stat[0:LO_ROWS, 3, :], stat[0:LO_ROWS, 2, :], ACT.Sqrt).then_inc(std_ready, 1)
            act.wait_ge(h_ready, 1)
            act.dma_start(h_dram[0:XP * NODES_P, :].rearrange("(p n) d -> p (n d)", n=NODES_P),
                          hn[0:XP, :, :].rearrange("p n d -> p (n d)")).then_inc(h_stored, 16)
            act.dma_start(h_dram[XP * NODES_P:N, :].rearrange("(p n) d -> p (n d)", n=XR),
                          hn[XP:XP + 1, 0:XR, :].rearrange("p n d -> p (n d)")).then_inc(h_stored, 16)

            def relu(i, kinds):
                for j, kind in enumerate(kinds):
                    if kind == MATMUL:
                        q = kinds[:j].count(MATMUL)
                        wait(act, scattered[j], i)
                        act.wait_ge(picked_ready[q], i + 1)
                        nc.scalar.activation(V[:, j, :, 1, :], picked[q][:, :, :], ACT.Relu,
                                             scale=1.0 / SCALE).then_inc(relu_done[q], 1)

            rounds(act, relu)

        @block.vector
        def _(dve):
            def tile_order(a):
                return a.rearrange("s (c p g) -> s c g p", c=HALVES, g=GRP)

            def in_order(a):
                return a.rearrange("s (c g p) -> s c g p", c=HALVES, g=GRP)

            dve.wait_ge(src_loaded, 48)
            nc.vector.tensor_scalar(lo_int[:, :], src_row[:, :], 2, None,
                                    ALU.logical_shift_right).then_inc(bits_ready, 1)
            nc.vector.tensor_scalar(b_int[:, :], src_row[:, :], BLK - 1, None, ALU.bitwise_and).then_inc(bits_ready, 1)
            dve.wait_ge(bits_ready, 2)
            for c in range(HALVES):
                last = nc.vector.tensor_copy(in_order(lo16[:, :])[:, c], tile_order(lo_int[:, :])[:, c])
            last.then_inc(lo_ready, 1)
            for c in range(HALVES):
                last = nc.vector.tensor_scalar(in_order(b16[:, :])[:, c], tile_order(b_int[:, :])[:, c], float(PARTS),
                                               float(PARTS * LO_ROWS), ALU.mult, ALU.add)
            last.then_inc(lo_ready, 1)

            step = [0]

            def link(ins):
                step[0] += 1
                ins.then_inc(dve_step, 1)
                dve.wait_ge(dve_step, step[0])

            L = LO_ROWS
            rows = [L, NODES_P, H]
            dve.wait_ge(x_loaded, 32)
            link(nc.vector.tensor_reduce(stat[0:L, 0, :], xs[0:L], AX.X, ALU.add))
            link(nc.vector.tensor_scalar(stat[0:L, 1, :], stat[0:L, 0, :], 1.0 / H, None, ALU.mult))
            link(nc.vector.tensor_tensor(xc[0:L], xs[0:L], stat[0:L, 1, :].unsqueeze(2).to_broadcast(rows), ALU.subtract))
            link(nc.vector.tensor_tensor(sq[0:L], xc[0:L], xc[0:L], ALU.mult))
            link(nc.vector.tensor_reduce(stat[0:L, 0, :], sq[0:L], AX.X, ALU.add))
            nc.vector.tensor_scalar(stat[0:L, 2, :], stat[0:L, 0, :], 1.0 / H, EPS, ALU.mult, ALU.add).then_inc(var_ready, 1)
            dve.wait_ge(std_ready, 1)
            link(nc.vector.reciprocal(stat[0:L, 4, :], stat[0:L, 3, :]))
            link(nc.vector.tensor_tensor(xc[0:L], xc[0:L], stat[0:L, 4, :].unsqueeze(2).to_broadcast(rows), ALU.mult))
            nc.vector.tensor_scalar(hn[0:L], xc[0:L], 0.0, None, ALU.max).then_inc(h_ready, 1)
            link(nc.vector.tensor_scalar(hs[0:L], xc[0:L], 0.0, SCALE, ALU.max, ALU.mult))
            dve.wait_ge(constants, 7)
            hi = h_hi[0:L].rearrange("p k (b d) -> p (k b) d", b=BLK)
            lo = h_lo[0:L].rearrange("p k (b d) -> p (k b) d", b=BLK)
            link(nc.vector.tensor_copy(hi, hs[0:L]))
            nc.vector.tensor_tensor(lo, hs[0:L], hi, ALU.subtract).then_inc(parts_ready, 1)

            turns = 0
            for what in ("dst", "weight", "src"):
                for c in range(HALVES):
                    turns += 1
                    dve.wait_ge(turns_done, turns)
                    got = turned[c][:, :, 0:NS]
                    tiles = slice(c * GRP, (c + 1) * GRP)
                    if what == "dst":
                        nc.vector.tensor_tensor(dst_w[:, :, 0, tiles].rearrange("p s t -> p t s"), got,
                                                base[:, :, tiles].rearrange("p s t -> p t s"),
                                                ALU.subtract).then_inc(turns_read, 1)
                    elif what == "weight":
                        nc.vector.tensor_copy(dst_w[:, :, 1, tiles].rearrange("p s t -> p t s"), got).then_inc(turns_read, 1)
                    else:
                        nc.vector.tensor_copy(src_t[:, :, tiles].rearrange("p s t -> p t s"), got).then_inc(turns_read, 1)
            dve.wait_ge(turns_read, 6)
            for g in range(GRP):
                last = nc.vector.memset(dst_w[0:(OVER - g + GRP - 1) // GRP, NS - 1, 1, g:g + 1], 0.0)
            last.then_inc(tables_ready, 1)
            dve.wait_ge(wcat_turned, 1)
            nc.vector.tensor_copy(w_cat_t[:, :], turned[0][:, 0, 0:H]).then_inc(wcat_ready, 1)
            link(nc.vector.memset(agg[:, :], 0.0))

            def add_acc(i, u, n):
                first = i * (len(KINDS) * STEP) + u * PER * STEP
                width = (n - 1) * STEP + HSTEP + WIN
                for j in range(u * PER, u * PER + n):
                    dve.wait_ge(scattered[j], i + 1)
                wait(dve, acc_added[1 - u], i + u)
                here = agg[:, bass.ds(first, width)]
                nc.vector.tensor_tensor(here, here, acc[u][:, 0:width], ALU.add).then_inc(acc_added[u], 1)

            def make(i, kinds):
                for j, kind in enumerate(kinds):
                    u = j // PER
                    if kind == MATMUL:
                        q = kinds[:j].count(MATMUL)
                        dve.wait_ge(lo_loaded[q], (i + 1) * 32)
                        if q >= 2:
                            dve.wait_ge(picked_ready[q - 2], i + 1)
                        else:
                            wait(dve, picked_ready[q + 2], i)
                        for k in range(PARTS):
                            last = nc.vector.tensor_scalar(one_hot[:, q % 2, k, :], lo_bc[:, q, :], lo_id[:, k:k + 1],
                                                           None, ALU.is_equal)
                        last.then_inc(onehot_ready[q], 1)
                    if j % PER == 0:
                        dve.wait_ge(dstw_staged[u], (i + 1) * 16)
                    wait(dve, scattered[j], i)
                    for t in range(TILES):
                        last = nc.vector.tensor_scalar(S[:, j, t, :], iota[:, 0:WIN], dst_w_now[:, u, j % PER, 0, t:t + 1],
                                                       dst_w_now[:, u, j % PER, 1, t:t + 1], ALU.is_equal, ALU.mult)
                    last.then_inc(S_ready[j], 1)
                    if j == PER - 1 and not (isinstance(i, int) and i == 0):
                        add_acc(i - 1, SETS - 1, PER)
                add_acc(i, 0, PER)

            rounds(dve, make)
            add_acc(FULL, 1, len(REST) - PER)

            where = dst_w[:, :, 0, :]
            nc.vector.tensor_reduce(reach[:, 0:1], where, AX.XY, ALU.max).then_inc(reach_ready, 1)
            nc.vector.tensor_reduce(reach[:, 1:2], where, AX.XY, ALU.min).then_inc(reach_ready, 1)
            dve.wait_ge(reach_ready, 2)
            nc.vector.tensor_scalar(reach[:, 2:3], reach[:, 0:1], WIN - 0.5, None, ALU.is_gt).then_inc(reach_ready, 1)
            dve.wait_ge(reach_ready, 3)
            nc.vector.scalar_tensor_tensor(reach[:, 3:4], reach[:, 1:2], -0.5, reach[:, 2:3], ALU.is_lt,
                                           ALU.max).then_inc(reach_ready, 1)
            dve.wait_ge(reach_summed, 1)
            nc.vector.tensor_copy(outside[:, :], turned[1][0:1, 0, 0:1]).then_inc(flag_ready, 1)
            dve.wait_ge(flag_ready, 1)
            dve.wait_ge(acc_added[0], FULL + 1)
            dve.wait_ge(acc_added[1], FULL + 1)
            with dve.If(dve.value_load(outside[0:1, 0:1], min_val=0, max_val=P) > 0):
                nc.vector.memset(agg[:, :], 0.0).then_inc(gen_added, 1)

                def sum_again(s, start):
                    dve.wait_ge(gen_dst, (s + 1) * 16)
                    nc.vector.tensor_tensor(dst_gen[:, BLOCKS, :], dst_w_now[:, 0, 0, 0, :],
                                            base[:, bass.ds(s, 1), :].rearrange("p s t -> p (s t)"),
                                            ALU.add).then_inc(gen_step, 1)
                    dve.wait_ge(gen_step, s * (BLOCKS + 1) + 1)
                    for b in range(BLOCKS):
                        nc.vector.tensor_scalar(dst_gen[:, b, :], dst_gen[:, BLOCKS, :], float(b * BANK), None,
                                                ALU.subtract).then_inc(gen_step, 1)
                    dve.wait_ge(gen_step, s * (BLOCKS + 1) + (BLOCKS + 1))
                    for b in range(BLOCKS):
                        width = min(BANK, N - b * BANK)
                        for t in range(TILES):
                            last = nc.vector.tensor_scalar(S_gen[:, t, 0:width], iota[:, 0:width], dst_gen[:, b, t:t + 1],
                                                           dst_w_now[:, 0, 0, 1, t:t + 1], ALU.is_equal, ALU.mult)
                        last.then_inc(gen_S, 1)
                        dve.wait_ge(gen_acc, s * BLOCKS + (b + 1))
                        dve.wait_ge(gen_added, s * BLOCKS + (b + 1))
                        here = agg[:, LEAD + b * BANK:LEAD + b * BANK + width]
                        nc.vector.tensor_tensor(here, here, acc[0][:, 0:width], ALU.add).then_inc(gen_added, 1)

                superchunks(dve, sum_again)
            dve.wait_ge(projected, 1)
            nc.vector.tensor_tensor(out_sb[:, :], turned[0][0:OP, :, :].rearrange("p a b -> p (a b)")[:, 0:OG * H],
                                    x_out[:, :], ALU.add).then_inc(out_ready, 1)

        @block.tensor
        def _(pe):
            pe.wait_ge(constants, 7)
            turns = 0
            for what, row in (("dst", dstf_row), ("weight", w_row), ("src", srcf_row)):
                if what == "dst":
                    pe.wait_ge(floats_ready, 2)
                if what == "weight":
                    pe.wait_ge(weight_loaded, 48)
                edges = row[:, :].rearrange("s (c p g) -> s c g p", c=HALVES, g=GRP)
                for c in range(HALVES):
                    wait(pe, turns_read, turns - 1)
                    turns += 1
                    for g in range(GRP):
                        last = nc.tensor.transpose(turned[c][:, g, 0:NS], edges[:, c, g, :], ident[0:NS, 0:NS])
                    last.then_inc(turns_done, 1)
            pe.wait_ge(turns_read, 6)
            pe.wait_ge(w_loaded, 96)
            nc.tensor.transpose(turned[0][:, 0, 0:H], w_cat[:, :], ident[0:H, 0:H]).then_inc(wcat_turned, 1)

            def pick(i, q):
                pe.wait_ge(onehot_ready[q], i + 1)
                wait(pe, relu_done[q], i)
                for t in range(TILES):
                    for k in range(PARTS):
                        edges = one_hot[:, q % 2, k, t * P:(t + 1) * P]
                        nc.tensor.matmul(picked[q][:, t, :], edges, h_hi[:, k, :], start=(k == 0), stop=False)
                        last = nc.tensor.matmul(picked[q][:, t, :], edges, h_lo[:, k, :], start=False,
                                                stop=(k == PARTS - 1))
                last.then_inc(picked_ready[q], 1)

            def scatter(i, j, kinds, first, last_of_set):
                u, q, r = j // PER, kinds[:j].count(MATMUL), kinds[:j].count(ROWS)
                if first:
                    wait(pe, acc_added[u], i)
                pe.wait_ge(attr_loaded[j], (i + 1) * (16 * HALVES))
                pe.wait_ge(S_ready[j], i + 1)
                if kinds[j] == MATMUL:
                    pe.wait_ge(relu_done[q], i + 1)
                else:
                    pe.wait_ge(rows_fetched[r], (i + 1) * (16 * TILES))
                for t in range(TILES):
                    at = (j % PER) * STEP + (t // GRP) * HSTEP
                    last = nc.tensor.matmul(acc[u][:, at:at + WIN], V[:, j, t, :, :].rearrange("p a f -> p (a f)"), S[:, j, t, :],
                                            start=first and t == 0, stop=last_of_set and t == TILES - 1,
                                            skip_group_check=True)
                last.then_inc(scattered[j], 1)

            pe.wait_ge(parts_ready, 1)
            pe.wait_ge(rings_zeroed, len(row_slots))

            def products(i, kinds):
                pick(i, 0)
                if not (isinstance(i, int) and i == 0):
                    scatter(i - 1, 5, KINDS, False, True)
                pick(i, 1)
                scatter(i, 0, kinds, True, False)
                scatter(i, 1, kinds, False, False)
                pick(i, 2)
                scatter(i, 2, kinds, False, True)
                if len(kinds) == len(KINDS):
                    pick(i, 3)
                    scatter(i, 3, kinds, True, False)
                    scatter(i, 4, kinds, False, False)
                else:
                    scatter(i, 4, kinds, True, False)
                    scatter(i, 3, kinds, False, True)

            rounds(pe, products)

            pe.wait_ge(reach_ready, 4)
            nc.tensor.matmul(turned[1][0:1, 0, 0:1], reach[:, 3:4], ones[:, :], start=True, stop=True).then_inc(reach_summed, 1)

            for u in range(SETS):
                pe.wait_ge(acc_added[u], FULL + 1)
            pe.wait_ge(flag_ready, 1)
            with pe.If(pe.value_load(outside[0:1, 0:1], min_val=0, max_val=P) > 0):
                def scatter_again(s, start):
                    pe.wait_ge(gen_attr, (s + 1) * (16 * HALVES))
                    pe.wait_ge(gen_rows, (s + 1) * (16 * TILES))
                    for b in range(BLOCKS):
                        width = min(BANK, N - b * BANK)
                        pe.wait_ge(gen_S, s * BLOCKS + (b + 1))
                        pe.wait_ge(gen_added, s * BLOCKS + (b + 1))
                        for t in range(TILES):
                            last = nc.tensor.matmul(acc[0][:, 0:width], V[:, 1, t, :, :].rearrange("p a f -> p (a f)"), S_gen[:, t, 0:width],
                                                    start=(t == 0), stop=(t == TILES - 1))
                        last.then_inc(gen_acc, 1)

                superchunks(pe, scatter_again)
                pe.wait_ge(gen_added, NS * BLOCKS + 1)

            pe.wait_ge(wcat_ready, 1)
            flat = turned[0][:, :, :].rearrange("p a b -> p (a b)")
            nodes = agg[:, LEAD:LEAD + N].rearrange("r (p j) -> r j p", j=OG)
            for j in range(OG):
                last = nc.tensor.matmul(flat[0:OP, j * H:(j + 1) * H], nodes[:, j, :], w_cat_t[:, :], start=True, stop=True)
            last.then_inc(projected, 1)


def build(nc, *args):
    gnn_kernel(nc, *args)

_INS = ['x','src','dst','edge_attr_64','edge_weight1','L0_gnn_W_node','L0_gnn_W_review']
_OUTS = [((3125, 16), 'float32')]

def kernel(**inputs):
    import numpy as _np
    import concourse.bacc as _bacc
    from concourse import mybir as _mybir
    from concourse.bass_utils import run_bass_kernel_spmd as _run

    nc = _bacc.Bacc("TRN2", target_bir_lowering=False, num_devices=1)
    arrays, args = {}, []
    for name in _INS:
        a = _np.ascontiguousarray(inputs[name])
        arrays[f"in_{name}_dram"] = a
        args.append(nc.dram_tensor(f"in_{name}_dram", a.shape, _mybir.dt.from_np(a.dtype), kind="ExternalInput").ap())
    for i, (shape, dtype) in enumerate(_OUTS):
        dt = _mybir.dt.from_np(_np.dtype(dtype))
        args.append(nc.dram_tensor(f"out_{i}_dram", shape, dt, kind="ExternalOutput").ap())
    build(nc, *args)
    r = _run(nc, [arrays], core_ids=[0])
    got = tuple(r.results[0][f"out_{i}_dram"] for i in range(len(_OUTS)))
    return got[0]
```

```python
import concourse.bass as bass
from concourse import mybir
from contextlib import ExitStack

F32, F16, I32 = mybir.dt.float32, mybir.dt.float16, mybir.dt.int32
ALU = mybir.AluOpType
ACT = mybir.ActivationFunctionType
AX = mybir.AxisListType

P = 128
H = 16
F = 64
HALVES, GRP = 2, 4
TILES = HALVES * GRP
HALF = GRP * P
SC = HALVES * HALF
WIN = 64
BLK = 4
PARTS = 7
LO_ROWS = 112
SCALE = 4096.0
MASK = -16384.0
EPS = 1e-5
MATMUL, ROWS = "matmul", "rows"
KINDS = [MATMUL, ROWS, MATMUL, MATMUL, ROWS, MATMUL, ROWS, MATMUL]
LAG = 2
SETS = 2
PER = len(KINDS) // SETS
BANK = 512


def gnn_kernel(nc, x, src, dst, attr, weight, w_node, w_review, out):
    N, E = x.shape[0], attr.shape[0]
    NS = -(-E // SC)
    OVER = NS * SC - E
    STEP = SC * N // E
    HSTEP = (STEP + 1) // 2
    LEAD = (WIN - HSTEP) // 2 - 1
    FULL = NS // len(KINDS)
    REST = KINDS[:NS - FULL * len(KINDS)]
    COLS = max((NS - 1) * STEP + HSTEP + WIN, LEAD + N)
    NODES_P = BLK * PARTS
    XP = N // NODES_P
    XR = N - XP * NODES_P
    OG = 25
    OP = N // OG
    RUNS = [(0, 64), (64, OP)]
    BLOCKS = -(-N // BANK)
    assert OG * OP == N and XP < LO_ROWS and LO_ROWS * NODES_P >= N

    lo_dram = nc.dram_tensor("lo_dram", (NS, SC), F16, kind="Internal").ap()
    b_dram = nc.dram_tensor("b_dram", (NS, SC), F16, kind="Internal").ap()
    h_dram = nc.dram_tensor("h_dram", (N, H), F32, kind="Internal").ap()

    G = F + H
    mm_slots = [j for j, kind in enumerate(KINDS) if kind == MATMUL]
    row_slots = [j for j, kind in enumerate(KINDS) if kind == ROWS]

    with ExitStack() as ctx:
        def sb(name, shape, dt):
            return ctx.enter_context(nc.sbuf_tensor(name, shape, dt))

        def pb(name, shape):
            return ctx.enter_context(nc.psum_tensor(name, shape, F32))

        def sem(name):
            return ctx.enter_context(nc.semaphore(name))

        ident = sb("ident", [P, P], F32)
        iota = sb("iota", [P, BANK], F32)
        window = sb("window", [P, WIN, TILES], F16)
        base = sb("base", [P, NS, TILES], F32)
        lo_id = sb("lo_id", [P, PARTS], F32)
        ones = sb("ones", [P, 1], F32)
        one = sb("one", [1, 2], F32)
        src_row = sb("src_row", [NS, SC], I32)
        dst_row = sb("dst_row", [NS, SC], I32)
        w_row = sb("w_row", [NS, SC], F32)
        lo16 = sb("lo16", [NS, SC], F16)
        b16 = sb("b16", [NS, SC], F16)
        dst_t = sb("dst_t", [P, NS, TILES], F32)
        dst16 = sb("dst16", [P, NS, TILES], F16)
        w_t = sb("w_t", [P, NS, TILES], F32)
        src_t = sb("src_t", [P, NS, TILES], I32)
        xs = sb("xs", [P, NODES_P, H], F32)
        xc = sb("xc", [P, NODES_P, H], F32)
        sq = sb("sq", [P, NODES_P, H], F32)
        hn = sb("hn", [P, NODES_P, H], F32)
        hs = sb("hs", [P, NODES_P, H], F32)
        stat = sb("stat", [P, 5, NODES_P], F32)
        h_hi = sb("h_hi", [P, PARTS, BLK * H], F16)
        h_lo = sb("h_lo", [P, PARTS, BLK * H], F16)
        x_out = sb("x_out", [64, len(RUNS), OG * H], F32)
        w_cat = sb("w_cat", [H, G], F32)
        w_cat_t = sb("w_cat_t", [G, H], F32)
        V = sb("V", [P, len(KINDS), TILES, G], F32)
        hit = sb("hit", [P, len(KINDS), WIN, TILES], F16)
        S = sb("S", [P, len(KINDS), TILES, WIN], F32)
        lo_bc = sb("lo_bc", [P, len(mm_slots), SC], F16)
        one_hot = sb("one_hot", [P, len(mm_slots), PARTS, SC], F16)
        spare = one_hot[0:NS, 3:5, :, :].rearrange("p a k e -> p (a k e)").bitcast(F32)
        srcf_row, dstf_row = spare[:, 0:SC], spare[:, SC:2 * SC]
        lo_int, b_int = spare[:, 2 * SC:3 * SC].bitcast(I32), spare[:, 3 * SC:4 * SC].bitcast(I32)
        unmasked = sb("unmasked", [P, len(mm_slots), TILES, BLK * H], F32)
        w_now = sb("w_now", [P, SETS, PER, TILES], F32)
        src_now = sb("src_now", [P, len(row_slots), TILES], I32)
        agg = sb("agg", [G, COLS], F32)
        reach = sb("reach", [P, 4], F32)
        outside = sb("outside", [1, 1], I32)
        out_sb = sb("out_sb", [64, len(RUNS), OG * H], F32)
        S_gen = one_hot[:, 0:2, :, :].rearrange("p a k e -> p (a k e)").bitcast(F32)[:, 0:TILES * BANK].rearrange(
            "p (t j) -> p t j", t=TILES)
        dst_gen = sb("dst_gen", [P, BLOCKS + 1, TILES], F32)

        picked = [pb(f"picked{q}", [P, TILES, BLK * H]) for q in range(len(mm_slots))]
        acc = [pb(f"acc{u}", [P, BANK]) for u in range(SETS)]
        small = pb("small", [P, GRP, P])
        turned = [small, picked[0].rearrange("p (g a) d -> p g (a d)", g=GRP)]

        x_loaded, w_loaded, xo_loaded = sem("x_loaded"), sem("w_loaded"), sem("xo_loaded")
        src_loaded, dst_loaded, weight_loaded = sem("src_loaded"), sem("dst_loaded"), sem("weight_loaded")
        x_zeroed, constants = sem("x_zeroed"), sem("constants")
        fills_done, bits_ready = sem("fills_done"), sem("bits_ready")
        one_ready, w_table_ready = sem("one_ready"), sem("w_table_ready")
        std_ready, var_ready = sem("std_ready"), sem("var_ready")
        h_ready, h_stored, parts_ready = sem("h_ready"), sem("h_stored"), sem("parts_ready")
        lo_ready, b_ready, lo_stored = sem("lo_ready"), sem("b_ready"), sem("lo_stored")
        floats_ready, turns_done, turns_read = sem("floats_ready"), sem("turns_done"), sem("turns_read")
        tables_ready = sem("tables_ready")
        src_table_ready, agg_cleared = sem("src_table_ready"), sem("agg_cleared")
        reach_ready, reach_summed, flag_ready = sem("reach_ready"), sem("reach_summed"), sem("flag_ready")
        wcat_turned, wcat_ready = sem("wcat_turned"), sem("wcat_ready")

        attr_loaded = [sem(f"attr_loaded{j}") for j in range(len(KINDS))]
        hit_ready = [sem(f"hit_ready{j}") for j in range(len(KINDS))]
        S_ready = [sem(f"S_ready{j}") for j in range(len(KINDS))]
        scattered = [sem(f"scattered{j}") for j in range(len(KINDS))]
        lo_loaded = [sem(f"lo_loaded{q}") for q in range(len(mm_slots))]
        onehot_ready = [sem(f"onehot_ready{q}") for q in range(len(mm_slots))]
        picked_ready = [sem(f"picked_ready{q}") for q in range(len(mm_slots))]
        relu_done = [sem(f"relu_done{q}") for q in range(len(mm_slots))]
        h_src_ready = [sem(f"h_src_ready{q}") for q in range(len(mm_slots))]
        w_staged = [sem(f"w_staged{u}") for u in range(SETS)]
        src_staged = [sem(f"src_staged{r}") for r in range(len(row_slots))]
        rows_fetched = [sem(f"rows_fetched{r}") for r in range(len(row_slots))]
        acc_added = [sem(f"acc_added{u}") for u in range(SETS)]
        dve_step, fetches_begun = sem("dve_step"), sem("fetches_begun")

        gen_step, gen_attr, gen_src, gen_rows = sem("gen_step"), sem("gen_attr"), sem("gen_src"), sem("gen_rows")
        gen_weights, gen_S, gen_acc, gen_added = sem("gen_weights"), sem("gen_S"), sem("gen_acc"), sem("gen_added")
        projected, out_ready, out_stored = sem("projected"), sem("out_ready"), sem("out_stored")

        def wait(eng, s, value):
            if not isinstance(value, int) or value > 0:
                eng.wait_ge(s, value)

        def rounds(eng, body, after_first=lambda: None, before_last=lambda: None):
            body(0, KINDS)
            after_first()
            with eng.Fori(1, FULL) as i:
                body(i, KINDS)
            before_last()
            body(FULL, REST)

        def edge_start(s):
            if isinstance(s, int):
                return min(s * SC, E - SC)
            return s * SC

        def superchunks(eng, body):
            with eng.Fori(0, NS - 1) as s:
                body(s, s * SC)
            body(NS - 1, E - SC)

        def load_rows(eng, row, flat, done):
            whole = flat[0:(NS - 1) * SC].rearrange("(s e) -> s e", e=SC)
            cut = (NS - 1) // 16 * 16
            eng.dma_start(row[0:cut, :], whole[0:cut, :]).then_inc(done, 16)
            eng.dma_start(row[cut:NS - 1, :], whole[cut:NS - 1, :]).then_inc(done, 16)
            eng.dma_start(row[NS - 1:NS, :], flat[E - SC:E].rearrange("(s e) -> s e", e=SC)).then_inc(done, 16)

        def load_attr(eng, j, first, done):
            for c in range(HALVES):
                eng.dma_start(V[:, j, c * GRP:(c + 1) * GRP, 0:F],
                              attr[bass.ds(first + c * HALF, HALF), :].rearrange("(p g) f -> p g f", g=GRP)
                              ).then_inc(done, 16)

        def turned_table(eng, n, table, done, copy):
            for c in range(HALVES):
                eng.wait_ge(turns_done, HALVES * n + c + 1)
                copy(table[:, :, c * GRP:(c + 1) * GRP].rearrange("p s t -> p t s"), turned[c][:, :, 0:NS]).then_inc(done, 1)

        block = ctx.enter_context(nc.Block())

        @block.sync
        def _(sp):
            load_rows(sp, src_row, src, src_loaded)
            sp.dma_start(w_cat[:, 0:F], w_review).then_inc(w_loaded, 16)
            sp.dma_start(w_cat[:, F:G], w_node).then_inc(w_loaded, 16)
            for n, (p0, p1) in enumerate(RUNS):
                sp.dma_start(x_out[0:p1 - p0, n, :], x.rearrange("(p j) d -> p (j d)", j=OG)[p0:p1, :]).then_inc(xo_loaded, 16)
            sp.wait_ge(lo_ready, 1)
            sp.dma_start(lo_dram, lo16[:, :]).then_inc(lo_stored, 16)
            sp.wait_ge(b_ready, 1)
            sp.dma_start(b_dram, b16[:, :]).then_inc(lo_stored, 16)

            def prefetch(i, kinds):
                for j, kind in enumerate(kinds):
                    first_round = isinstance(i, int) and i == 0
                    s = i * len(KINDS) + j
                    u, q, r = j // PER, kinds[:j].count(MATMUL), kinds[:j].count(ROWS)
                    if kind == ROWS:
                        if first_round and r == 0:
                            sp.wait_ge(src_table_ready, HALVES)
                        wait(sp, rows_fetched[r], i * (16 * TILES))
                        sp.dma_start(src_now[:, r, :], src_t[:, bass.ds(s, 1), :].rearrange("p s t -> p (s t)")
                                     ).then_inc(src_staged[r], 16)
                    else:
                        if first_round and q == 0:
                            sp.wait_ge(lo_stored, 32)
                        wait(sp, onehot_ready[q], i)
                        sp.dma_start(lo_bc[0:LO_ROWS, q, :],
                                     lo_dram[bass.ds(s, 1), :].to_broadcast([LO_ROWS, SC])
                                     ).then_inc(lo_loaded[q], 16)
                        sp.dma_start(lo_bc[LO_ROWS:P, q, :],
                                     b_dram[bass.ds(s, 1), :].to_broadcast([P - LO_ROWS, SC])
                                     ).then_inc(lo_loaded[q], 16)
                    if j % PER == 0:
                        wait(sp, S_ready[(u + 1) * PER - 1], i)
                    wait(sp, scattered[j], i)
                    load_attr(sp, j, edge_start(s), attr_loaded[j])
                    if j == (PER - 1 if first_round and u == 0 else u * PER):
                        if first_round and u == 0:
                            sp.wait_ge(tables_ready, 1)
                        n = min(PER, len(kinds) - u * PER)
                        sp.dma_start(w_now[:, u, 0:n, :].rearrange("p s t -> p (s t)"),
                                     w_t[:, bass.ds(i * len(KINDS) + u * PER, n), :].rearrange("p s t -> p (s t)")
                                     ).then_inc(w_staged[u], 16)

            rounds(sp, prefetch)

            sp.wait_ge(flag_ready, 1)
            with sp.If(sp.value_load(outside[0:1, 0:1], min_val=0, max_val=P) > 0):
                def load_again(s, start):
                    sp.wait_ge(gen_added, s * BLOCKS + 1)
                    load_attr(sp, 1, start, gen_attr)
                    sp.dma_start(src_now[:, 0, :], src_t[:, bass.ds(s, 1), :].rearrange("p s t -> p (s t)")
                                 ).then_inc(gen_src, 16)
                    sp.dma_start(w_now[:, 0, 0, :], w_t[:, bass.ds(s, 1), :].rearrange("p s t -> p (s t)")
                                 ).then_inc(gen_weights, 16)

                superchunks(sp, load_again)

            stores = 0
            for n, (p0, p1) in enumerate(RUNS):
                sp.wait_ge(out_ready, n + 1)
                cut = p0 + (p1 - p0) // 16 * 16
                for a, b in ((p0, cut), (cut, p1)):
                    if a < b:
                        sp.dma_start(out.rearrange("(p j) d -> p (j d)", j=OG)[a:b, :],
                                     out_sb[a - p0:b - p0, n, :]).then_inc(out_stored, 16)
                        stores += 16
            sp.wait_ge(out_stored, stores)

        @block.gpsimd
        def _(pool):
            nc.gpsimd.memset(xs[:, :, :], 0.0).then_inc(x_zeroed, 1)
            nc.gpsimd.iota(lo_id[:, :], [[1, PARTS]], base=0, channel_multiplier=PARTS,
                           allow_small_or_imprecise_dtypes=True).then_inc(constants, 1)
            nc.gpsimd.memset(ident[:, :], 1.0).then_inc(fills_done, 1)
            nc.gpsimd.memset(h_hi[:, 1:PARTS, :], 0.0).then_inc(fills_done, 1)
            pool.wait_ge(fills_done, 2)
            nc.gpsimd.memset(h_hi[:, 0, :], MASK).then_inc(fills_done, 1)
            nc.gpsimd.affine_select(out=ident[:, :], in_=ident[:, :], compare_op=ALU.is_equal, fill=0.0, base=0,
                                    pattern=[[-1, P]], channel_multiplier=1).then_inc(constants, 1)
            pool.wait_ge(fills_done, 3)
            masks = h_hi[:, 0, :].rearrange("p (b d) -> p b d", b=BLK)
            nc.gpsimd.affine_select(out=masks, in_=masks, compare_op=ALU.not_equal, fill=0.0, base=-LO_ROWS,
                                    pattern=[[-1, BLK], [0, H]], channel_multiplier=1).then_inc(constants, 1)
            nc.gpsimd.memset(h_lo[:, :, :], 0.0).then_inc(constants, 1)
            nc.gpsimd.iota(iota[:, :], [[1, BANK]], base=0, channel_multiplier=0,
                           allow_small_or_imprecise_dtypes=True).then_inc(constants, 1)
            nc.gpsimd.iota(window[:, :, :], [[1, WIN], [0, TILES]], base=0, channel_multiplier=0,
                           allow_small_or_imprecise_dtypes=True).then_inc(constants, 1)
            nc.gpsimd.iota(base[:, :, :], [[STEP, NS], [HSTEP, HALVES], [0, GRP]], base=-LEAD, channel_multiplier=0,
                           allow_small_or_imprecise_dtypes=True).then_inc(constants, 1)
            nc.gpsimd.memset(ones[:, :], 1.0).then_inc(constants, 1)
            nc.gpsimd.memset(agg[:, :], 0.0).then_inc(agg_cleared, 1)

            def fetch_rows(i, kinds):
                for j, kind in enumerate(kinds):
                    if kind == ROWS:
                        r = kinds[:j].count(ROWS)
                        wait(pool, scattered[j], i)
                        pool.wait_ge(src_staged[r], (i + 1) * 16)
                        pool.sem_inc(fetches_begun, 1)
                        for t in range(TILES):
                            pool.indirect_dma_start(V[:, j, t, F:G], None, h_dram,
                                                    bass.IndirectOffsetOnAxis(src_now[:, r, t:t + 1], 0)
                                                    ).then_inc(rows_fetched[r], 16)

            pool.wait_ge(h_stored, 32)
            rounds(pool, fetch_rows)

            pool.wait_ge(flag_ready, 1)
            with pool.If(pool.value_load(outside[0:1, 0:1], min_val=0, max_val=P) > 0):
                def fetch_again(s, start):
                    pool.wait_ge(gen_added, s * BLOCKS + 1)
                    pool.wait_ge(gen_src, (s + 1) * 16)
                    pool.sem_inc(fetches_begun, 1)
                    for t in range(TILES):
                        pool.indirect_dma_start(V[:, 1, t, F:G], None, h_dram,
                                                bass.IndirectOffsetOnAxis(src_now[:, 0, t:t + 1], 0)
                                                ).then_inc(gen_rows, 16)

                superchunks(pool, fetch_again)

        @block.scalar
        def _(act):
            act.wait_ge(x_zeroed, 1)
            act.dma_start(xs[0:XP, :, :].rearrange("p n d -> p (n d)"),
                          x[0:XP * NODES_P, :].rearrange("(p n) d -> p (n d)", n=NODES_P)).then_inc(x_loaded, 16)
            act.dma_start(xs[XP:XP + 1, 0:XR, :].rearrange("p n d -> p (n d)"),
                          x[XP * NODES_P:N, :].rearrange("(p n) d -> p (n d)", n=XR)).then_inc(x_loaded, 16)
            load_rows(act, dst_row, dst, dst_loaded)
            load_rows(act, w_row, weight.rearrange("e one -> (e one)"), weight_loaded)
            act.wait_ge(one_ready, 1)
            nc.scalar.activation(one[:, 1:2], one[:, 0:1], ACT.Sqrt)
            act.wait_ge(src_loaded, 48)
            nc.scalar.activation(srcf_row[:, :], src_row[:, :], ACT.Copy).then_inc(floats_ready, 1)
            act.wait_ge(dst_loaded, 48)
            nc.scalar.activation(dstf_row[:, :], dst_row[:, :], ACT.Copy).then_inc(floats_ready, 1)
            act.wait_ge(var_ready, 1)
            nc.scalar.activation(stat[0:LO_ROWS, 3, :], stat[0:LO_ROWS, 2, :], ACT.Sqrt).then_inc(std_ready, 1)
            turned_table(act, 0, src_t, src_table_ready, nc.scalar.copy)
            act.wait_ge(h_ready, 1)
            act.dma_start(h_dram[0:XP * NODES_P, :].rearrange("(p n) d -> p (n d)", n=NODES_P),
                          hn[0:XP, :, :].rearrange("p n d -> p (n d)")).then_inc(h_stored, 16)
            act.dma_start(h_dram[XP * NODES_P:N, :].rearrange("(p n) d -> p (n d)", n=XR),
                          hn[XP:XP + 1, 0:XR, :].rearrange("p n d -> p (n d)")).then_inc(h_stored, 16)

            turned_table(act, 2, w_t, w_table_ready, nc.scalar.copy)

            def weigh(i, j):
                if j % PER == 0:
                    act.wait_ge(w_staged[j // PER], (i + 1) * 16)
                act.wait_ge(hit_ready[j], i + 1)
                wait(act, scattered[j], i)
                for t in range(TILES):
                    last = nc.scalar.activation(S[:, j, t, :], hit[:, j, :, t], ACT.Copy,
                                                scale=w_now[:, j // PER, j % PER, t:t + 1])
                last.then_inc(S_ready[j], 1)

            def relu(i, q):
                act.wait_ge(picked_ready[q], i + 1)
                wait(act, h_src_ready[q], i)
                nc.scalar.activation(unmasked[:, q, :, :], picked[q][:, :, :], ACT.Relu,
                                     scale=1.0 / SCALE).then_inc(relu_done[q], 1)

            def weigh_and_relu(i, kinds):
                weigh(i, 0)
                for j, kind in enumerate(kinds):
                    if kind == MATMUL:
                        relu(i, kinds[:j].count(MATMUL))
                    if j + 1 < len(kinds):
                        weigh(i, j + 1)

            rounds(act, weigh_and_relu)

        @block.vector
        def _(dve):
            nc.vector.memset(one[:, :], 1.0).then_inc(one_ready, 1)
            step = [0]

            def link(ins):
                step[0] += 1
                ins.then_inc(dve_step, 1)
                dve.wait_ge(dve_step, step[0])

            L = LO_ROWS
            rows = [L, NODES_P, H]
            dve.wait_ge(x_loaded, 32)
            link(nc.vector.tensor_reduce(stat[0:L, 0, :], xs[0:L], AX.X, ALU.add))
            link(nc.vector.tensor_scalar(stat[0:L, 1, :], stat[0:L, 0, :], 1.0 / H, None, ALU.mult))
            link(nc.vector.tensor_tensor(xc[0:L], xs[0:L], stat[0:L, 1, :].unsqueeze(2).to_broadcast(rows), ALU.subtract))
            link(nc.vector.tensor_tensor(sq[0:L], xc[0:L], xc[0:L], ALU.mult))
            link(nc.vector.tensor_reduce(stat[0:L, 0, :], sq[0:L], AX.X, ALU.add))
            nc.vector.tensor_scalar(stat[0:L, 2, :], stat[0:L, 0, :], 1.0 / H, EPS, ALU.mult, ALU.add).then_inc(var_ready, 1)

            def tile_order(a, c):
                return a.rearrange("s (c p g) -> s c g p", c=HALVES, g=GRP)[:, c]

            def in_order(a, c):
                return a.rearrange("s (c g p) -> s c g p", c=HALVES, g=GRP)[:, c]

            dve.wait_ge(src_loaded, 48)
            nc.vector.tensor_scalar(lo_int, src_row[:, :], 2, None, ALU.logical_shift_right).then_inc(bits_ready, 1)
            nc.vector.tensor_scalar(b_int, src_row[:, :], BLK - 1, None, ALU.bitwise_and).then_inc(bits_ready, 1)
            dve.wait_ge(bits_ready, 1)
            for c in range(HALVES):
                last = nc.vector.tensor_copy(in_order(lo16[:, :], c), tile_order(lo_int, c))
            last.then_inc(lo_ready, 1)
            dve.wait_ge(bits_ready, 2)
            for c in range(HALVES):
                last = nc.vector.tensor_scalar(in_order(b16[:, :], c), tile_order(b_int, c), float(PARTS),
                                               float(PARTS * LO_ROWS), ALU.mult, ALU.add)
            last.then_inc(b_ready, 1)

            dve.wait_ge(std_ready, 1)
            link(nc.vector.reciprocal(stat[0:L, 4, :], stat[0:L, 3, :]))
            link(nc.vector.tensor_tensor(xc[0:L], xc[0:L], stat[0:L, 4, :].unsqueeze(2).to_broadcast(rows), ALU.mult))
            nc.vector.tensor_scalar(hn[0:L], xc[0:L], 0.0, None, ALU.max).then_inc(h_ready, 1)
            link(nc.vector.tensor_scalar(hs[0:L], xc[0:L], 0.0, SCALE, ALU.max, ALU.mult))
            dve.wait_ge(constants, 8)
            hi = h_hi[0:L].rearrange("p k (b d) -> p (k b) d", b=BLK)
            lo = h_lo[0:L].rearrange("p k (b d) -> p (k b) d", b=BLK)
            link(nc.vector.tensor_copy(hi, hs[0:L]))
            nc.vector.tensor_tensor(lo, hs[0:L], hi, ALU.subtract).then_inc(parts_ready, 1)

            for c in range(HALVES):
                dve.wait_ge(turns_done, HALVES + c + 1)
                tiles = slice(c * GRP, (c + 1) * GRP)
                nc.vector.tensor_tensor(dst_t[:, :, tiles].rearrange("p s t -> p t s"), turned[c][:, :, 0:NS],
                                        base[:, :, tiles].rearrange("p s t -> p t s"), ALU.subtract).then_inc(turns_read, 1)
            dve.wait_ge(turns_read, 2)
            link(nc.vector.tensor_copy(dst16[:, :, :], dst_t[:, :, :]))

            def make_weights_table():
                dve.wait_ge(w_table_ready, 2)
                for g in range(GRP):
                    last = nc.vector.memset(w_t[0:(OVER - g + GRP - 1) // GRP, NS - 1, g:g + 1], 0.0)
                last.then_inc(tables_ready, 1)
                dve.wait_ge(wcat_turned, 1)
                nc.vector.tensor_copy(w_cat_t[:, :], turned[0][0:G, 0, 0:H]).then_inc(wcat_ready, 1)

            def add_acc(i, u, n):
                first = i * (len(KINDS) * STEP) + u * PER * STEP
                width = (n - 1) * STEP + HSTEP + WIN
                for j in range(u * PER, u * PER + n):
                    dve.wait_ge(scattered[j], i + 1)
                if isinstance(i, int) and i == 0 and u == 0:
                    dve.wait_ge(agg_cleared, 1)
                wait(dve, acc_added[1 - u], i + u)
                here = agg[:, bass.ds(first, width)]
                nc.vector.tensor_tensor(here, here, acc[u][0:G, 0:width], ALU.add).then_inc(acc_added[u], 1)

            def make_one_hot(i, q):
                dve.wait_ge(lo_loaded[q], (i + 1) * 32)
                wait(dve, picked_ready[q], i)
                for k in range(PARTS):
                    last = nc.vector.tensor_scalar(one_hot[:, q, k, :], lo_bc[:, q, :], lo_id[:, k:k + 1],
                                                   None, ALU.is_equal)
                last.then_inc(onehot_ready[q], 1)

            def find_hits(i, j):
                wait(dve, S_ready[j], i)
                nc.vector.tensor_tensor(hit[:, j, :, :], window[:, :, :],
                                        dst16[:, bass.ds(i * len(KINDS) + j, 1), :].to_broadcast([P, WIN, TILES]),
                                        ALU.is_equal).then_inc(hit_ready[j], 1)

            def add_blocks(i, q):
                dve.wait_ge(relu_done[q], i + 1)
                wait(dve, scattered[mm_slots[q]], i)
                nc.vector.tensor_reduce(V[:, mm_slots[q], :, F:G],
                                        unmasked[:, q, :, :].rearrange("p t (b d) -> p t d b", b=BLK),
                                        AX.X, ALU.add).then_inc(h_src_ready[q], 1)

            def make(i, kinds):
                first_round = isinstance(i, int) and i == 0
                for j, kind in enumerate(kinds):
                    if kind == MATMUL:
                        q = kinds[:j].count(MATMUL)
                        make_one_hot(i, q)
                        if first_round and q == 0:
                            make_weights_table()
                    find_hits(i, j)
                    if kind == MATMUL:
                        if q >= LAG:
                            add_blocks(i, q - LAG)
                        elif not first_round:
                            add_blocks(i - 1, q - LAG + len(mm_slots))
                    if j == PER - 1 and not first_round:
                        add_acc(i - 1, SETS - 1, PER)
                if len(kinds) < len(KINDS):
                    for q in range(kinds.count(MATMUL) - LAG, kinds.count(MATMUL)):
                        add_blocks(i, q)
                add_acc(i, 0, PER)

            def find_reach():
                nc.vector.tensor_reduce(reach[:, 0:1], dst_t[:, :, :], AX.XY, ALU.max).then_inc(reach_ready, 1)
                nc.vector.tensor_reduce(reach[:, 1:2], dst_t[:, :, :], AX.XY, ALU.min).then_inc(reach_ready, 1)
                dve.wait_ge(reach_ready, 2)
                nc.vector.tensor_scalar(reach[:, 2:3], reach[:, 0:1], WIN - 0.5, None, ALU.is_gt).then_inc(reach_ready, 1)
                dve.wait_ge(reach_ready, 3)
                nc.vector.scalar_tensor_tensor(reach[:, 3:4], reach[:, 1:2], -0.5, reach[:, 2:3], ALU.is_lt,
                                               ALU.max).then_inc(reach_ready, 1)

            def set_flag():
                dve.wait_ge(reach_summed, 1)
                nc.vector.tensor_copy(outside[:, :], small[0:1, 1, 0:1]).then_inc(flag_ready, 1)

            rounds(dve, make, after_first=find_reach, before_last=set_flag)
            add_acc(FULL, 1, len(REST) - PER)
            dve.wait_ge(flag_ready, 1)
            dve.wait_ge(acc_added[0], FULL + 1)
            dve.wait_ge(acc_added[1], FULL + 1)
            with dve.If(dve.value_load(outside[0:1, 0:1], min_val=0, max_val=P) > 0):
                nc.vector.memset(agg[:, :], 0.0).then_inc(gen_added, 1)

                def sum_again(s, start):
                    dve.wait_ge(gen_weights, (s + 1) * 16)
                    nc.vector.tensor_tensor(dst_gen[:, BLOCKS, :], dst_t[:, bass.ds(s, 1), :].rearrange("p s t -> p (s t)"),
                                            base[:, bass.ds(s, 1), :].rearrange("p s t -> p (s t)"),
                                            ALU.add).then_inc(gen_step, 1)
                    dve.wait_ge(gen_step, s * (BLOCKS + 1) + 1)
                    for b in range(BLOCKS):
                        nc.vector.tensor_scalar(dst_gen[:, b, :], dst_gen[:, BLOCKS, :], float(b * BANK), None,
                                                ALU.subtract).then_inc(gen_step, 1)
                    dve.wait_ge(gen_step, s * (BLOCKS + 1) + (BLOCKS + 1))
                    for b in range(BLOCKS):
                        width = min(BANK, N - b * BANK)
                        for t in range(TILES):
                            last = nc.vector.tensor_scalar(S_gen[:, t, 0:width], iota[:, 0:width], dst_gen[:, b, t:t + 1],
                                                           w_now[:, 0, 0, t:t + 1], ALU.is_equal, ALU.mult)
                        last.then_inc(gen_S, 1)
                        dve.wait_ge(gen_acc, s * BLOCKS + (b + 1))
                        dve.wait_ge(gen_added, s * BLOCKS + (b + 1))
                        here = agg[:, LEAD + b * BANK:LEAD + b * BANK + width]
                        nc.vector.tensor_tensor(here, here, acc[0][0:G, 0:width], ALU.add).then_inc(gen_added, 1)

                superchunks(dve, sum_again)
            dve.wait_ge(xo_loaded, 16 * len(RUNS))
            for n, (p0, p1) in enumerate(RUNS):
                dve.wait_ge(projected, n + 1)
                nc.vector.tensor_tensor(out_sb[0:p1 - p0, n, :], turned[n][0:p1 - p0, :, :].rearrange("p a b -> p (a b)")[:, 0:OG * H],
                                        x_out[0:p1 - p0, n, :], ALU.add).then_inc(out_ready, 1)

        @block.tensor
        def _(pe):
            pe.wait_ge(constants, 2)
            for what, row in (("src", srcf_row), ("dst", dstf_row), ("weight", w_row)):
                if what == "src":
                    pe.wait_ge(floats_ready, 1)
                elif what == "dst":
                    pe.wait_ge(floats_ready, 2)
                else:
                    pe.wait_ge(weight_loaded, 48)
                edges = row[:, :].rearrange("s (c p g) -> s c g p", c=HALVES, g=GRP)
                for c in range(HALVES):
                    if what == "dst":
                        pe.wait_ge(src_table_ready, c + 1)
                    elif what == "weight":
                        pe.wait_ge(turns_read, c + 1)
                    for g in range(GRP):
                        last = nc.tensor.transpose(turned[c][:, g, 0:NS], edges[:, c, g, :], ident[0:NS, 0:NS])
                    last.then_inc(turns_done, 1)
            pe.wait_ge(w_table_ready, HALVES)
            pe.wait_ge(w_loaded, 32)
            nc.tensor.transpose(turned[0][0:G, 0, 0:H], w_cat[:, :], ident[0:H, 0:H]).then_inc(wcat_turned, 1)

            def pick(i, q):
                pe.wait_ge(onehot_ready[q], i + 1)
                wait(pe, relu_done[q], i)
                for t in range(TILES):
                    for k in range(PARTS):
                        edges = one_hot[:, q, k, t * P:(t + 1) * P]
                        nc.tensor.matmul(picked[q][:, t, :], edges, h_hi[:, k, :], start=(k == 0), stop=False)
                        last = nc.tensor.matmul(picked[q][:, t, :], edges, h_lo[:, k, :], start=False,
                                                stop=(k == PARTS - 1))
                last.then_inc(picked_ready[q], 1)

            def scatter(i, j, last_of_set):
                u, q, r = j // PER, KINDS[:j].count(MATMUL), KINDS[:j].count(ROWS)
                if j % PER == 0:
                    wait(pe, acc_added[u], i)
                pe.wait_ge(attr_loaded[j], (i + 1) * (16 * HALVES))
                pe.wait_ge(S_ready[j], i + 1)
                if KINDS[j] == MATMUL:
                    pe.wait_ge(h_src_ready[q], i + 1)
                else:
                    pe.wait_ge(rows_fetched[r], (i + 1) * (16 * TILES))
                for t in range(TILES):
                    at = (j % PER) * STEP + (t // GRP) * HSTEP
                    last = nc.tensor.matmul(acc[u][0:G, at:at + WIN], V[:, j, t, :], S[:, j, t, :],
                                            start=(j % PER == 0 and t == 0), stop=(last_of_set and t == TILES - 1),
                                            skip_group_check=True)
                last.then_inc(scattered[j], 1)

            pe.wait_ge(parts_ready, 1)

            def products(i, kinds):
                done = 0
                for j, kind in enumerate(kinds):
                    if kind == MATMUL:
                        pick(i, kinds[:j].count(MATMUL))
                        if j == 0 and not (isinstance(i, int) and i == 0):
                            for late in range(mm_slots[-1], len(KINDS)):
                                scatter(i - 1, late, late == len(KINDS) - 1)
                        for ready in range(done, j):
                            scatter(i, ready, ready % PER == PER - 1)
                        done = j
                if len(kinds) < len(KINDS):
                    for ready in range(done, len(kinds)):
                        scatter(i, ready, ready in (PER - 1, len(kinds) - 1))

            def sum_reach():
                pe.wait_ge(reach_ready, 4)
                pe.wait_ge(wcat_ready, 1)
                nc.tensor.matmul(small[0:1, 1, 0:1], reach[:, 3:4], ones[:, :], start=True,
                                 stop=True).then_inc(reach_summed, 1)

            flag = []

            def read_flag():
                pe.wait_ge(flag_ready, 1)
                flag.append(pe.value_load(outside[0:1, 0:1], min_val=0, max_val=P))

            rounds(pe, products, after_first=sum_reach, before_last=read_flag)

            for u in range(SETS):
                pe.wait_ge(acc_added[u], FULL + 1)
            with pe.If(flag[0] > 0):
                def scatter_again(s, start):
                    pe.wait_ge(gen_attr, (s + 1) * (16 * HALVES))
                    pe.wait_ge(gen_rows, (s + 1) * (16 * TILES))
                    for b in range(BLOCKS):
                        width = min(BANK, N - b * BANK)
                        pe.wait_ge(gen_S, s * BLOCKS + (b + 1))
                        pe.wait_ge(gen_added, s * BLOCKS + (b + 1))
                        for t in range(TILES):
                            last = nc.tensor.matmul(acc[0][0:G, 0:width], V[:, 1, t, :], S_gen[:, t, 0:width],
                                                    start=(t == 0), stop=(t == TILES - 1))
                        last.then_inc(gen_acc, 1)

                superchunks(pe, scatter_again)
                pe.wait_ge(gen_added, NS * BLOCKS + 1)

            pe.wait_ge(wcat_ready, 1)
            nodes = agg[:, LEAD:LEAD + N].rearrange("r (p j) -> r j p", j=OG)
            for n, (p0, p1) in enumerate(RUNS):
                flat = turned[n].rearrange("p a b -> p (a b)")
                for j in range(OG):
                    last = nc.tensor.matmul(flat[0:p1 - p0, j * H:(j + 1) * H], nodes[:, j, p0:p1], w_cat_t[:, :],
                                            start=True, stop=True)
                last.then_inc(projected, 1)


def build(nc, *args):
    gnn_kernel(nc, *args)

_INS = ['x','src','dst','edge_attr_64','edge_weight1','L0_gnn_W_node','L0_gnn_W_review']
_OUTS = [((3125, 16), 'float32')]

def kernel(**inputs):
    import numpy as _np
    import concourse.bacc as _bacc
    from concourse import mybir as _mybir
    from concourse.bass_utils import run_bass_kernel_spmd as _run

    nc = _bacc.Bacc("TRN2", target_bir_lowering=False, num_devices=1)
    arrays, args = {}, []
    for name in _INS:
        a = _np.ascontiguousarray(inputs[name])
        arrays[f"in_{name}_dram"] = a
        args.append(nc.dram_tensor(f"in_{name}_dram", a.shape, _mybir.dt.from_np(a.dtype), kind="ExternalInput").ap())
    for i, (shape, dtype) in enumerate(_OUTS):
        dt = _mybir.dt.from_np(_np.dtype(dtype))
        args.append(nc.dram_tensor(f"out_{i}_dram", shape, dt, kind="ExternalOutput").ap())
    build(nc, *args)
    r = _run(nc, [arrays], core_ids=[0])
    got = tuple(r.results[0][f"out_{i}_dram"] for i in range(len(_OUTS)))
    return got[0]
```

```python
import concourse.bass as bass
from concourse import mybir
from contextlib import ExitStack

F32, F16, I32 = mybir.dt.float32, mybir.dt.float16, mybir.dt.int32
ALU = mybir.AluOpType
ACT = mybir.ActivationFunctionType
AX = mybir.AxisListType

P = 128
H = 16
F = 64
HALVES, GRP = 2, 4
TILES = HALVES * GRP
HALF = GRP * P
SC = HALVES * HALF
WIN = 64
BLK = 5
PARTS = 5
LO_ROWS = 125
ROUND_IT = 1.5 * 2 ** 23
SCALE = 4096.0
MASK = -16384.0
EPS = 1e-5
MATMUL, ROWS = "matmul", "rows"
KINDS = [MATMUL, ROWS, MATMUL] * 3
LAST_KINDS = [ROWS, ROWS] + KINDS[2:]
LAG = 2
AHEAD = 2
SETS = 3
RING = 3
WARM_UP = 30
BANKS = 4
PER = len(KINDS) // SETS
BANK = 512


def gnn_kernel(nc, x, src, dst, attr, weight, w_node, w_review, out):
    N, E = x.shape[0], attr.shape[0]
    NS = -(-E // SC)
    OVER = NS * SC - E
    STEP = SC * N // E
    HSTEP = (STEP + 1) // 2
    LEAD = (WIN - HSTEP) // 2 - 1
    FULL = NS // len(KINDS)
    REST = LAST_KINDS[:NS - FULL * len(KINDS)]
    assert REST == [ROWS, ROWS] and LAG == AHEAD == 2 and SETS == 3
    COLS = max((NS - 1) * STEP + HSTEP + WIN, LEAD + N)
    NODES_P = BLK * PARTS
    X_SPLIT = LO_ROWS // 16 * 16
    RUNS = [(0, 96), (96, LO_ROWS)]
    BLOCKS = -(-N // BANK)
    assert (FULL * len(KINDS) - PER) * STEP - LEAD >= RUNS[-1][0] * NODES_P
    assert LO_ROWS * NODES_P == N and LO_ROWS + 1 <= P and BLK == PARTS

    def by_node(a):
        return a.rearrange("(p n) d -> p (n d)", n=NODES_P)

    lo_b_dram = nc.dram_tensor("lo_b_dram", (NS, 2 * SC), F16, kind="Internal").ap()
    h_dram = nc.dram_tensor("h_dram", (N, H), F32, kind="Internal").ap()

    G = F + H
    mm_slots = [j for j, kind in enumerate(KINDS) if kind == MATMUL]
    row_slots = [j for j, kind in enumerate(KINDS) if kind == ROWS]

    with ExitStack() as ctx:
        def sb(name, shape, dt):
            return ctx.enter_context(nc.sbuf_tensor(name, shape, dt))

        def pb(name, shape):
            return ctx.enter_context(nc.psum_tensor(name, shape, F32))

        def sem(name):
            return ctx.enter_context(nc.semaphore(name))

        ident = sb("ident", [P, P], F32)
        iota = sb("iota", [P, BANK], F32)
        window = sb("window", [P, WIN, TILES], F16)
        less_base = sb("less_base", [NS, HALVES], F32)
        lo_id = sb("lo_id", [P, PARTS], F32)
        ones = sb("ones", [P, 1], F32)
        one = sb("one", [1, 2], F32)
        src_row = sb("src_row", [NS, SC], I32)
        dst_row = sb("dst_row", [NS, SC], I32)
        w_row = sb("w_row", [NS, SC], F32)
        lo_b = sb("lo_b", [NS, 2 * SC], F16)
        lo16, b16 = lo_b[:, 0:SC], lo_b[:, SC:2 * SC]
        dst_t = sb("dst_t", [P, NS, TILES], F32)
        dst16 = sb("dst16", [P, NS, TILES], F16)
        w_t = sb("w_t", [P, NS, TILES], F32)
        src_t = sb("src_t", [P, NS, TILES], I32)
        xs = sb("xs", [P, NODES_P, H], F32)
        xc = sb("xc", [P, NODES_P, H], F32)
        sq = sb("sq", [P, NODES_P, H], F32)
        hn = sb("hn", [P, NODES_P, H], F32)
        hs = sb("hs", [P, NODES_P, H], F32)
        stat = sb("stat", [P, 5, NODES_P], F32)
        h_hi = sb("h_hi", [P, PARTS, BLK * H], F16)
        h_lo = sb("h_lo", [P, PARTS, BLK * H], F16)
        w_cat = sb("w_cat", [H, G], F32)
        w_cat_t = sb("w_cat_t", [G, H], F32)
        V = sb("V", [P, len(KINDS), TILES, G], F32)
        hit = sb("hit", [P, len(KINDS), WIN, TILES], F16)
        S = sb("S", [P, len(KINDS), TILES, WIN], F32)
        lo_bc = sb("lo_bc", [P, len(mm_slots), SC], F16)
        one_hot = sb("one_hot", [P, RING, PARTS, SC], F16)
        spare = one_hot[0:NS, 1:3, :, :].rearrange("p a k e -> p (a k e)").bitcast(F32)
        srcf_row, dstf_row = spare[:, 0:SC], spare[:, SC:2 * SC]
        fifth, lo_row = spare[:, 2 * SC:3 * SC], spare[:, 3 * SC:4 * SC]
        unmasked = sb("unmasked", [P, RING, TILES, BLK * H], F32)
        w_now = sb("w_now", [P, SETS, PER, TILES], F32)
        src_now = sb("src_now", [P, len(row_slots), TILES], I32)
        agg = sb("agg", [G, COLS], F32)
        reach = sb("reach", [P, 4], F32)
        outside = sb("outside", [1, 1], I32)
        out_sb = sb("out_sb", [P, NODES_P * H], F32)
        S_gen = one_hot[:, 0:2, :, :].rearrange("p a k e -> p (a k e)").bitcast(F32)[:, 0:TILES * BANK].rearrange(
            "p (t j) -> p t j", t=TILES)
        base = sb("base", [P, NS, TILES], F32)
        dst_gen = sb("dst_gen", [P, BLOCKS + 1, TILES], F32)

        picked_bank = [pb(f"picked{n}", [P, BANK]) for n in range(BANKS)]
        acc = [pb(f"acc{u}", [P, BANK]) for u in range(SETS)]
        small = pb("small", [P, GRP, P])
        def quarters(bank):
            return bank[:, :].rearrange("p (g e) -> p g e", g=GRP)

        w_turned = [quarters(acc[0]), quarters(acc[1])]
        src_turned = [small[:, :, :], quarters(picked_bank[0])]
        dst_turned = [quarters(acc[2]), quarters(picked_bank[1])]
        projected_bank = [small[:, :, :].rearrange("p a b -> p (a b)")] * (len(RUNS) - 1) + [picked_bank[0]]
        wcat_turned = small[0:G, 0, NS:NS + H]

        x_loaded, w_loaded, less_base_ready = sem("x_loaded"), sem("w_loaded"), sem("less_base_ready")
        src_loaded, dst_loaded, weight_loaded = sem("src_loaded"), sem("dst_loaded"), sem("weight_loaded")
        constants = sem("constants")
        fills_done = sem("fills_done")
        one_ready, w_table_ready = sem("one_ready"), sem("w_table_ready")
        std_ready, var_ready = sem("std_ready"), sem("var_ready")
        h_ready, h_stored, parts_ready = sem("h_ready"), sem("h_stored"), sem("parts_ready")
        fifth_ready, lo_row_ready = sem("fifth_ready"), sem("lo_row_ready")
        lo_ready, b_ready, lo_stored = sem("lo_ready"), sem("b_ready"), sem("lo_stored")
        src_floats, dst_floats = sem("src_floats"), sem("dst_floats")
        w_turns, src_turns, dst_turns = sem("w_turns"), sem("src_turns"), sem("dst_turns")
        dst16_ready, dst_table_ready, repeats_cleared = sem("dst16_ready"), sem("dst_table_ready"), sem("repeats_cleared")
        src_table_ready, agg_cleared = sem("src_table_ready"), sem("agg_cleared")
        reach_ready, reach_summed, flag_ready = sem("reach_ready"), sem("reach_summed"), sem("flag_ready")
        wcat_turns, wcat_ready = sem("wcat_turns"), sem("wcat_ready")

        attr_loaded = [sem(f"attr_loaded{j}") for j in range(len(KINDS))]
        hit_ready = [sem(f"hit_ready{j}") for j in range(len(KINDS))]
        S_ready = [sem(f"S_ready{j}") for j in range(len(KINDS))]
        scattered = [sem(f"scattered{j}") for j in range(len(KINDS))]
        lo_loaded = [sem(f"lo_loaded{q}") for q in range(len(mm_slots))]
        onehot_ready = [sem(f"onehot_ready{q}") for q in range(len(mm_slots))]
        picked_ready = [sem(f"picked_ready{q}") for q in range(len(mm_slots))]
        relu_done = [sem(f"relu_done{q}") for q in range(len(mm_slots))]
        h_src_ready = [sem(f"h_src_ready{q}") for q in range(len(mm_slots))]
        w_staged = [sem(f"w_staged{u}") for u in range(SETS)]
        src_staged = [sem(f"src_staged{r}") for r in range(len(row_slots))]
        rows_fetched = [sem(f"rows_fetched{r}") for r in range(len(row_slots))]
        acc_added = [sem(f"acc_added{u}") for u in range(SETS)]
        dve_step, fetches_begun = sem("dve_step"), sem("fetches_begun")

        base_ready = sem("base_ready")
        gen_step, gen_attr, gen_src, gen_rows = sem("gen_step"), sem("gen_attr"), sem("gen_src"), sem("gen_rows")
        gen_weights, gen_S, gen_acc, gen_added = sem("gen_weights"), sem("gen_S"), sem("gen_acc"), sem("gen_added")
        gen_projected = sem("gen_projected")
        projected, out_ready, out_stored = sem("projected"), sem("out_ready"), sem("out_stored")

        def wait(eng, s, value):
            if not isinstance(value, int) or value > 0:
                eng.wait_ge(s, value)

        def rounds(eng, body, after_first=lambda: None, before_last=lambda: None, last_body=None):
            body(0, KINDS)
            after_first()
            with eng.Fori(1, FULL) as i:
                body(i, KINDS)
            before_last()
            (last_body or body)(FULL, REST)

        def edge_start(s):
            if isinstance(s, int):
                return min(s * SC, E - SC)
            return s * SC

        def superchunks(eng, body):
            with eng.Fori(0, NS - 1) as s:
                body(s, s * SC)
            body(NS - 1, E - SC)

        def load_rows(eng, row, flat, done):
            eng.dma_start(row[0:NS - 1, :], flat[0:(NS - 1) * SC].rearrange("(s e) -> s e", e=SC)).then_inc(done, 16)
            eng.dma_start(row[NS - 1:NS, :], flat[E - SC:E].rearrange("(s e) -> s e", e=SC)).then_inc(done, 16)

        def load_attr(eng, j, first, done):
            for c in range(HALVES):
                eng.dma_start(V[:, j, c * GRP:(c + 1) * GRP, 0:F],
                              attr[bass.ds(first + c * HALF, HALF), :].rearrange("(p g) f -> p g f", g=GRP)
                              ).then_inc(done, 16)

        def tile_order(a, c):
            return a.rearrange("s (c p g) -> s c g p", c=HALVES, g=GRP)[:, c]

        def in_order(a, c):
            return a.rearrange("s (c g p) -> s c g p", c=HALVES, g=GRP)[:, c]

        def picked(q, c):
            return picked_bank[(HALVES * q + c) % BANKS][:, 0:GRP * BLK * H].rearrange("p (g d) -> p g d", g=GRP)

        def earlier(i, q, back):
            return (i, q - back) if q >= back else (i - 1, q - back + len(mm_slots))


        block = ctx.enter_context(nc.Block())

        @block.sync
        def _(sp):
            load_rows(sp, src_row, src, src_loaded)
            load_rows(sp, dst_row, dst, dst_loaded)
            load_rows(sp, w_row, weight.rearrange("e one -> (e one)"), weight_loaded)
            sp.dma_start(w_cat[:, 0:F], w_review).then_inc(w_loaded, 16)
            sp.dma_start(w_cat[:, F:G], w_node).then_inc(w_loaded, 16)

            def stage_src(s, r):
                sp.dma_start(src_now[:, r, :], src_t[:, bass.ds(s, 1), :].rearrange("p s t -> p (s t)")
                             ).then_inc(src_staged[r], 16)

            sp.wait_ge(lo_ready, HALVES)
            sp.wait_ge(b_ready, 1)
            sp.dma_start(lo_b_dram, lo_b[:, :]).then_inc(lo_stored, 16)
            sp.wait_ge(src_table_ready, HALVES)
            stage_src(row_slots[0], 0)

            def spread(s, q):
                sp.dma_start(lo_bc[0:LO_ROWS, q, :],
                             lo_b_dram[bass.ds(s, 1), 0:SC].to_broadcast([LO_ROWS, SC])
                             ).then_inc(lo_loaded[q], 16)
                sp.dma_start(lo_bc[LO_ROWS:P, q, :],
                             lo_b_dram[bass.ds(s, 1), SC:2 * SC].to_broadcast([P - LO_ROWS, SC])
                             ).then_inc(lo_loaded[q], 16)

            sp.wait_ge(h_ready, 1)
            h_rows = hn[:, :, :].rearrange("p n d -> p (n d)")
            sp.dma_start(by_node(h_dram)[0:X_SPLIT], h_rows[0:X_SPLIT]).then_inc(h_stored, 16)
            sp.dma_start(by_node(h_dram)[X_SPLIT:LO_ROWS], h_rows[X_SPLIT:LO_ROWS]).then_inc(h_stored, 16)
            sp.wait_ge(lo_stored, 16)
            for q in range(2):
                spread(mm_slots[q], q)

            def prefetch(i, kinds):
                for j, kind in enumerate(kinds):
                    first_round = isinstance(i, int) and i == 0
                    s = i * len(KINDS) + j
                    u, q = j // PER, kinds[:j].count(MATMUL)
                    for ahead in ([j] if j == 0 else []) + [j + 1]:
                        if ahead < len(kinds) and kinds[ahead] == ROWS and not (first_round and ahead == row_slots[0]):
                            to = kinds[:ahead].count(ROWS)
                            wait(sp, rows_fetched[to], i * (16 * TILES))
                            stage_src(i * len(KINDS) + ahead, to)
                    if kind == MATMUL and not (first_round and q < 2):
                        wait(sp, onehot_ready[q], i)
                        spread(s, q)
                    if j % PER == 0:
                        wait(sp, S_ready[(u + 1) * PER - 1], i)
                    wait(sp, scattered[j], i)
                    load_attr(sp, j, edge_start(s), attr_loaded[j])
                    if j == u * PER:
                        if first_round and u == 0:
                            sp.wait_ge(w_table_ready, 2)
                            sp.wait_ge(repeats_cleared, 1)
                        n = min(PER, len(kinds) - u * PER)
                        sp.dma_start(w_now[:, u, 0:n, :].rearrange("p s t -> p (s t)"),
                                     w_t[:, bass.ds(i * len(KINDS) + u * PER, n), :].rearrange("p s t -> p (s t)")
                                     ).then_inc(w_staged[u], 16)

            rounds(sp, prefetch)

            sp.wait_ge(flag_ready, 1)
            with sp.If(sp.value_load(outside[0:1, 0:1], min_val=0, max_val=P) > 0):
                def load_again(s, start):
                    sp.wait_ge(gen_added, s * BLOCKS + 1)
                    load_attr(sp, 1, start, gen_attr)
                    sp.dma_start(src_now[:, 0, :], src_t[:, bass.ds(s, 1), :].rearrange("p s t -> p (s t)")
                                 ).then_inc(gen_src, 16)
                    sp.dma_start(w_now[:, 0, 0, :], w_t[:, bass.ds(s, 1), :].rearrange("p s t -> p (s t)")
                                 ).then_inc(gen_weights, 16)

                superchunks(sp, load_again)

            for n, (p0, p1) in enumerate(RUNS):
                sp.wait_ge(out_ready, n + 1)
                sp.dma_start(by_node(out)[p0:p1, :], out_sb[p0:p1, :]).then_inc(out_stored, 16)
            sp.wait_ge(out_stored, 16 * len(RUNS))

        @block.gpsimd
        def _(pool):
            nc.gpsimd.iota(lo_id[:, :], [[1, PARTS]], base=0, channel_multiplier=PARTS,
                           allow_small_or_imprecise_dtypes=True).then_inc(constants, 1)
            nc.gpsimd.memset(ident[:, :], 1.0).then_inc(fills_done, 1)
            nc.gpsimd.memset(h_hi[:, :, :], MASK).then_inc(fills_done, 1)
            nc.gpsimd.iota(less_base[:, :], [[-HSTEP, HALVES]], base=LEAD, channel_multiplier=-STEP,
                           allow_small_or_imprecise_dtypes=True).then_inc(less_base_ready, 1)
            pool.wait_ge(fills_done, 2)
            nc.gpsimd.affine_select(out=ident[:, :], in_=ident[:, :], compare_op=ALU.is_equal, fill=0.0, base=0,
                                    pattern=[[-1, P]], channel_multiplier=1).then_inc(constants, 1)
            masks = h_hi[:, :, :].rearrange("p k (b d) -> p k b d", b=BLK)
            nc.gpsimd.affine_select(out=masks, in_=masks, compare_op=ALU.not_equal, fill=0.0, base=0,
                                    pattern=[[1, PARTS], [-1, BLK], [0, H]], channel_multiplier=0).then_inc(constants, 1)
            nc.gpsimd.memset(h_lo[:, :, :], 0.0).then_inc(constants, 1)
            nc.gpsimd.iota(iota[:, :], [[1, BANK]], base=0, channel_multiplier=0,
                           allow_small_or_imprecise_dtypes=True).then_inc(constants, 1)
            nc.gpsimd.iota(window[:, :, :], [[1, WIN], [0, TILES]], base=0, channel_multiplier=0,
                           allow_small_or_imprecise_dtypes=True).then_inc(constants, 1)
            nc.gpsimd.memset(ones[:, :], 1.0).then_inc(constants, 1)
            nc.gpsimd.memset(agg[:, :], 0.0).then_inc(agg_cleared, 1)

            def fetch_rows(i, kinds):
                for j, kind in enumerate(kinds):
                    if kind == ROWS:
                        r = kinds[:j].count(ROWS)
                        wait(pool, scattered[j], i)
                        pool.wait_ge(src_staged[r], (i + 1) * 16)
                        pool.sem_inc(fetches_begun, 1)
                        for t in range(TILES):
                            pool.indirect_dma_start(V[:, j, t, F:G], None, h_dram,
                                                    bass.IndirectOffsetOnAxis(src_now[:, r, t:t + 1], 0)
                                                    ).then_inc(rows_fetched[r], 16)

            pool.wait_ge(h_stored, 32)
            rounds(pool, fetch_rows)

            pool.wait_ge(flag_ready, 1)
            with pool.If(pool.value_load(outside[0:1, 0:1], min_val=0, max_val=P) > 0):
                nc.gpsimd.iota(base[:, :, :], [[STEP, NS], [HSTEP, HALVES], [0, GRP]], base=-LEAD, channel_multiplier=0,
                               allow_small_or_imprecise_dtypes=True).then_inc(base_ready, 1)

                def fetch_again(s, start):
                    pool.wait_ge(gen_added, s * BLOCKS + 1)
                    pool.wait_ge(gen_src, (s + 1) * 16)
                    pool.sem_inc(fetches_begun, 1)
                    for t in range(TILES):
                        pool.indirect_dma_start(V[:, 1, t, F:G], None, h_dram,
                                                bass.IndirectOffsetOnAxis(src_now[:, 0, t:t + 1], 0)
                                                ).then_inc(gen_rows, 16)

                superchunks(pool, fetch_again)

        @block.scalar
        def _(act):
            xs_rows = xs[:, :, :].rearrange("p n d -> p (n d)")
            act.dma_start(xs_rows[0:X_SPLIT], by_node(x)[0:X_SPLIT]).then_inc(x_loaded, 16)
            act.dma_start(xs_rows[X_SPLIT:LO_ROWS], by_node(x)[X_SPLIT:LO_ROWS]).then_inc(x_loaded, 16)
            act.wait_ge(one_ready, 1)
            nc.scalar.activation(one[:, 1:2], one[:, 0:1], ACT.Sqrt)

            def table_half(table, c, turned, done):
                nc.scalar.copy(table[:, :, c * GRP:(c + 1) * GRP].rearrange("p s t -> p t s"), turned[c][:, :, 0:NS]
                               ).then_inc(done, 1)

            act.wait_ge(src_loaded, 32)
            nc.scalar.activation(fifth, src_row[:, :], ACT.Copy, scale=1.0 / BLK,
                                 bias=-(BLK - 1) / (2.0 * BLK) - LO_ROWS).then_inc(fifth_ready, 1)
            nc.scalar.activation(srcf_row[:, :], src_row[:, :], ACT.Copy).then_inc(src_floats, 1)
            act.wait_ge(lo_row_ready, 1)
            for c in range(HALVES):
                nc.scalar.activation(in_order(lo16, c), tile_order(lo_row, c), ACT.Copy,
                                     bias=float(LO_ROWS)).then_inc(lo_ready, 1)
            for c in range(HALVES):
                act.wait_ge(src_turns, c + 1)
                table_half(src_t, c, src_turned, src_table_ready)
            act.wait_ge(var_ready, 1)
            nc.scalar.activation(stat[0:LO_ROWS, 3, :], stat[0:LO_ROWS, 2, :], ACT.Sqrt).then_inc(std_ready, 1)
            act.wait_ge(dst_loaded, 32)
            act.wait_ge(less_base_ready, 1)
            for c in range(HALVES):
                nc.scalar.activation(dstf_row[:, c * HALF:(c + 1) * HALF], dst_row[:, c * HALF:(c + 1) * HALF],
                                     ACT.Identity, bias=less_base[:, c:c + 1]).then_inc(dst_floats, 1)
            for c in range(HALVES):
                act.wait_ge(w_turns, c + 1)
                table_half(w_t, c, w_turned, w_table_ready)
            for c in range(HALVES):
                act.wait_ge(dst_turns, c + 1)
                table_half(dst16, c, dst_turned, dst16_ready)
            for c in range(HALVES):
                table_half(dst_t, c, dst_turned, dst_table_ready)

            def weigh(i, j):
                if j % PER == 0:
                    act.wait_ge(w_staged[j // PER], (i + 1) * 16)
                act.wait_ge(hit_ready[j], i + 1)
                wait(act, scattered[j], i)
                for t in range(TILES):
                    last = nc.scalar.activation(S[:, j, t, :], hit[:, j, :, t], ACT.Copy,
                                                scale=w_now[:, j // PER, j % PER, t:t + 1])
                last.then_inc(S_ready[j], 1)

            def relu(i, q):
                wait(act, h_src_ready[earlier(i, q, RING)[1]], earlier(i, q, RING)[0] + 1)
                for c in range(HALVES):
                    act.wait_ge(picked_ready[q], i * HALVES + (c + 1))
                    nc.scalar.activation(unmasked[:, q % RING, c * GRP:(c + 1) * GRP, :], picked(q, c), ACT.Relu,
                                         scale=1.0 / SCALE).then_inc(relu_done[q], 1)

            def relu_and_weigh(i, kinds):
                first_round = isinstance(i, int) and i == 0
                if first_round:
                    weigh(i, 0)
                for j, kind in enumerate(kinds):
                    if kind == MATMUL:
                        relu(i, kinds[:j].count(MATMUL))
                    if first_round and j == 0:
                        for early in range(1, AHEAD):
                            weigh(i, early)
                    if j + AHEAD < len(kinds):
                        weigh(i, j + AHEAD)
                    elif len(kinds) == len(KINDS):
                        weigh(i + 1, j + AHEAD - len(kinds))

            rounds(act, relu_and_weigh)

        @block.vector
        def _(dve):
            nc.vector.memset(one[:, :], 1.0).then_inc(one_ready, 1)
            step = [0]

            def link(ins):
                step[0] += 1
                ins.then_inc(dve_step, 1)
                dve.wait_ge(dve_step, step[0])

            L = LO_ROWS
            rows = [L, NODES_P, H]
            dve.wait_ge(x_loaded, 32)
            link(nc.vector.tensor_reduce(stat[0:L, 0, :], xs[0:L], AX.X, ALU.add))
            link(nc.vector.scalar_tensor_tensor(xc[0:L], stat[0:L, 0, :].unsqueeze(2).to_broadcast(rows), 1.0 / H,
                                                xs[0:L], ALU.mult, ALU.subtract))
            dve.wait_ge(fifth_ready, 1)
            nc.vector.tensor_scalar(lo_row, fifth, ROUND_IT, ROUND_IT, ALU.add, ALU.subtract).then_inc(lo_row_ready, 1)
            dve.wait_ge(lo_row_ready, 1)
            for c in range(HALVES):
                last = nc.vector.scalar_tensor_tensor(in_order(b16, c), tile_order(lo_row, c), float(-BLK),
                                                      tile_order(src_row[:, :], c), ALU.mult, ALU.add)
            last.then_inc(b_ready, 1)
            link(nc.vector.tensor_tensor(sq[0:L], xc[0:L], xc[0:L], ALU.mult))
            link(nc.vector.tensor_reduce(stat[0:L, 0, :], sq[0:L], AX.X, ALU.add))
            nc.vector.tensor_scalar(stat[0:L, 2, :], stat[0:L, 0, :], 1.0 / H, EPS, ALU.mult, ALU.add).then_inc(var_ready, 1)

            dve.wait_ge(std_ready, 1)
            link(nc.vector.reciprocal(stat[0:L, 4, :], stat[0:L, 3, :]))
            link(nc.vector.scalar_tensor_tensor(sq[0:L], stat[0:L, 4, :].unsqueeze(2).to_broadcast(rows), -1.0,
                                                xc[0:L], ALU.mult, ALU.mult))
            nc.vector.tensor_scalar(hn[0:L], sq[0:L], 0.0, None, ALU.max).then_inc(h_ready, 1)
            link(nc.vector.tensor_scalar(hs[0:L], sq[0:L], 0.0, SCALE, ALU.max, ALU.mult))
            dve.wait_ge(constants, 7)
            hi = h_hi[0:L].rearrange("p k (b d) -> p (k b) d", b=BLK)
            lo = h_lo[0:L].rearrange("p k (b d) -> p (k b) d", b=BLK)
            link(nc.vector.tensor_copy(hi, hs[0:L]))
            nc.vector.tensor_tensor(lo, hs[0:L], hi, ALU.subtract).then_inc(parts_ready, 1)

            dve.wait_ge(w_table_ready, HALVES)
            for g in range(GRP):
                last = nc.vector.memset(w_t[0:(OVER - g + GRP - 1) // GRP, NS - 1, g:g + 1], 0.0)
            last.then_inc(repeats_cleared, 1)

            def add_acc(i, u, before, n=PER):
                first = i * (len(KINDS) * STEP) + u * PER * STEP
                width = (n - 1) * STEP + HSTEP + WIN
                for j in range(u * PER, u * PER + n):
                    dve.wait_ge(scattered[j], i + 1)
                if isinstance(i, int) and i == 0 and u == 0:
                    dve.wait_ge(agg_cleared, 1)
                if before:
                    dve.wait_ge(acc_added[before[1]], before[0] + 1)
                here = agg[:, bass.ds(first, width)]
                nc.vector.tensor_tensor(here, here, acc[u][0:G, 0:width], ALU.add).then_inc(acc_added[u], 1)

            def make_one_hot(i, q):
                dve.wait_ge(lo_loaded[q], (i + 1) * 32)
                then, there = earlier(i, q, RING)
                wait(dve, picked_ready[there], then * HALVES + HALVES)
                for k in range(PARTS):
                    last = nc.vector.tensor_scalar(one_hot[:, q % RING, k, :], lo_bc[:, q, :], lo_id[:, k:k + 1],
                                                   None, ALU.is_equal)
                last.then_inc(onehot_ready[q], 1)

            def find_hits(i, j):
                wait(dve, S_ready[j], i)
                nc.vector.tensor_tensor(hit[:, j, :, :], window[:, :, :],
                                        dst16[:, bass.ds(i * len(KINDS) + j, 1), :].to_broadcast([P, WIN, TILES]),
                                        ALU.is_equal).then_inc(hit_ready[j], 1)

            def add_blocks(i, q):
                dve.wait_ge(relu_done[q], i * HALVES + HALVES)
                wait(dve, scattered[mm_slots[q]], i)
                nc.vector.tensor_reduce(V[:, mm_slots[q], :, F:G],
                                        unmasked[:, q % RING, :, :].rearrange("p t (b d) -> p t d b", b=BLK),
                                        AX.X, ALU.add).then_inc(h_src_ready[q], 1)

            def make(i, kinds):
                first_round = isinstance(i, int) and i == 0
                for j, kind in enumerate(kinds):
                    if kind == MATMUL:
                        q = kinds[:j].count(MATMUL)
                        if first_round and q in (LAG, LAG + 1):
                            add_blocks(i, q - LAG)
                        make_one_hot(i, q)
                    if first_round and j == 0:
                        dve.wait_ge(dst16_ready, HALVES)
                    find_hits(i, j)
                    if kind == MATMUL and not (first_round and q <= LAG + 1):
                        add_blocks(*earlier(i, q, LAG))
                    if j % PER == 0 and not (first_round and j < 2 * PER):
                        this, before = j // PER - 2, j // PER - 3
                        add_acc(i + this // SETS, this % SETS,
                                None if first_round and this == 0 else (i + before // SETS, before % SETS))

            def make_last(i, kinds):
                for j in range(len(kinds)):
                    find_hits(i, j)
                add_blocks(i - 1, len(mm_slots) - 2)
                add_acc(i - 1, SETS - 2, (i - 1, SETS - 3))
                add_blocks(i - 1, len(mm_slots) - 1)
                add_acc(i - 1, SETS - 1, (i - 1, SETS - 2))
                add_acc(i, 0, (i - 1, SETS - 1), len(kinds))

            def find_reach():
                dve.wait_ge(wcat_turns, 1)
                nc.vector.tensor_copy(w_cat_t[:, :], wcat_turned).then_inc(wcat_ready, 1)
                dve.wait_ge(dst_table_ready, HALVES)
                nc.vector.tensor_reduce(reach[:, 0:1], dst_t[:, :, :], AX.XY, ALU.max).then_inc(reach_ready, 1)
                nc.vector.tensor_reduce(reach[:, 1:2], dst_t[:, :, :], AX.XY, ALU.min).then_inc(reach_ready, 1)
                dve.wait_ge(reach_ready, 2)
                nc.vector.tensor_scalar(reach[:, 2:3], reach[:, 0:1], WIN - 0.5, None, ALU.is_gt).then_inc(reach_ready, 1)
                dve.wait_ge(reach_ready, 3)
                nc.vector.scalar_tensor_tensor(reach[:, 3:4], reach[:, 1:2], -0.5, reach[:, 2:3], ALU.is_lt,
                                               ALU.max).then_inc(reach_ready, 1)

            def set_flag():
                dve.wait_ge(reach_summed, 1)
                nc.vector.tensor_copy(outside[:, :], small[0:1, 1, 0:1]).then_inc(flag_ready, 1)

            rounds(dve, make, after_first=find_reach, before_last=set_flag, last_body=make_last)
            dve.wait_ge(flag_ready, 1)
            dve.wait_ge(acc_added[0], FULL + 1)
            with dve.If(dve.value_load(outside[0:1, 0:1], min_val=0, max_val=P) > 0):
                nc.vector.memset(agg[:, :], 0.0).then_inc(gen_added, 1)
                dve.wait_ge(base_ready, 1)

                def sum_again(s, start):
                    dve.wait_ge(gen_weights, (s + 1) * 16)
                    nc.vector.tensor_tensor(dst_gen[:, BLOCKS, :], dst_t[:, bass.ds(s, 1), :].rearrange("p s t -> p (s t)"),
                                            base[:, bass.ds(s, 1), :].rearrange("p s t -> p (s t)"),
                                            ALU.add).then_inc(gen_step, 1)
                    dve.wait_ge(gen_step, s * (BLOCKS + 1) + 1)
                    for b in range(BLOCKS):
                        nc.vector.tensor_scalar(dst_gen[:, b, :], dst_gen[:, BLOCKS, :], float(b * BANK), None,
                                                ALU.subtract).then_inc(gen_step, 1)
                    dve.wait_ge(gen_step, s * (BLOCKS + 1) + (BLOCKS + 1))
                    for b in range(BLOCKS):
                        width = min(BANK, N - b * BANK)
                        for t in range(TILES):
                            last = nc.vector.tensor_scalar(S_gen[:, t, 0:width], iota[:, 0:width], dst_gen[:, b, t:t + 1],
                                                           w_now[:, 0, 0, t:t + 1], ALU.is_equal, ALU.mult)
                        last.then_inc(gen_S, 1)
                        dve.wait_ge(gen_acc, s * BLOCKS + (b + 1))
                        dve.wait_ge(gen_added, s * BLOCKS + (b + 1))
                        here = agg[:, LEAD + b * BANK:LEAD + b * BANK + width]
                        nc.vector.tensor_tensor(here, here, acc[0][0:G, 0:width], ALU.add).then_inc(gen_added, 1)

                superchunks(dve, sum_again)
                dve.wait_ge(gen_projected, 1)
            for n, (p0, p1) in enumerate(RUNS):
                dve.wait_ge(projected, n + 1)
                nc.vector.tensor_tensor(out_sb[p0:p1], projected_bank[n][p0:p1, 0:NODES_P * H],
                                        xs[p0:p1].rearrange("p n d -> p (n d)"), ALU.add).then_inc(out_ready, 1)

        @block.tensor
        def _(pe):
            pe.wait_ge(constants, 2)

            def turn(row, c, turned, done):
                edges = row[:, c * HALF:(c + 1) * HALF].rearrange("s (p g) -> s g p", g=GRP)
                for g in range(GRP):
                    last = nc.tensor.transpose(turned[c][:, g, 0:NS], edges[:, g, :], ident[0:NS, 0:NS])
                last.then_inc(done, 1)

            pe.wait_ge(src_floats, 1)
            for c in range(HALVES):
                turn(srcf_row, c, src_turned, src_turns)
            pe.wait_ge(weight_loaded, 32)
            for c in range(HALVES):
                turn(w_row, c, w_turned, w_turns)
            for c in range(HALVES):
                pe.wait_ge(dst_floats, c + 1)
                turn(dstf_row, c, dst_turned, dst_turns)
            pe.wait_ge(w_loaded, 32)
            nc.tensor.transpose(wcat_turned, w_cat[:, :], ident[0:H, 0:H]).then_inc(wcat_turns, 1)

            for _ in range(WARM_UP):
                nc.tensor.transpose(picked_bank[BANKS - 1][:, 0:P], ident[:, :], ident[:, :])

            def pick(i, q):
                pe.wait_ge(onehot_ready[q], i + 1)
                then, there = earlier(i, q, BANKS // HALVES)
                for c in range(HALVES):
                    wait(pe, relu_done[there], then * HALVES + (c + 1))
                    for g in range(GRP):
                        t = c * GRP + g
                        for k in range(PARTS):
                            edges = one_hot[:, q % RING, k, t * P:(t + 1) * P]
                            nc.tensor.matmul(picked(q, c)[:, g, :], edges, h_hi[:, k, :], start=(k == 0), stop=False)
                            last = nc.tensor.matmul(picked(q, c)[:, g, :], edges, h_lo[:, k, :], start=False,
                                                    stop=(k == PARTS - 1))
                    last.then_inc(picked_ready[q], 1)

            def scatter(i, j, kinds=KINDS):
                u, q, r = j // PER, kinds[:j].count(MATMUL), kinds[:j].count(ROWS)
                last_of_set = j % PER == PER - 1 or j == len(kinds) - 1
                if j % PER == 0:
                    wait(pe, acc_added[u], i)
                pe.wait_ge(attr_loaded[j], (i + 1) * (16 * HALVES))
                pe.wait_ge(S_ready[j], i + 1)
                if kinds[j] == MATMUL:
                    pe.wait_ge(h_src_ready[q], i + 1)
                else:
                    pe.wait_ge(rows_fetched[r], (i + 1) * (16 * TILES))
                for t in range(TILES):
                    at = (j % PER) * STEP + (t // GRP) * HSTEP
                    last = nc.tensor.matmul(acc[u][0:G, at:at + WIN], V[:, j, t, :], S[:, j, t, :],
                                            start=(j % PER == 0 and t == 0), stop=(last_of_set and t == TILES - 1),
                                            skip_group_check=True)
                last.then_inc(scattered[j], 1)

            pe.wait_ge(parts_ready, 1)
            pe.wait_ge(w_table_ready, HALVES)
            pe.wait_ge(src_table_ready, HALVES)
            pe.wait_ge(dst_table_ready, HALVES)

            def scatter_late(i):
                for j in range(mm_slots[-1], len(KINDS)):
                    scatter(i, j)

            def products(i, kinds):
                done = 0
                for j, kind in enumerate(kinds):
                    if kind == MATMUL:
                        pick(i, kinds[:j].count(MATMUL))
                        if j == 0 and not (isinstance(i, int) and i == 0):
                            scatter_late(i - 1)
                        for ready in range(done, j):
                            scatter(i, ready)
                        done = j

            nodes = agg[:, LEAD:LEAD + N].rearrange("r (p j) -> r j p", j=NODES_P)

            def project(n):
                for p0 in range(*RUNS[n], 64):
                    p1 = min(p0 + 64, RUNS[n][1])
                    for j in range(NODES_P):
                        last = nc.tensor.matmul(projected_bank[n][p0:p1, j * H:(j + 1) * H], nodes[:, j, p0:p1],
                                                w_cat_t[:, :], start=True, stop=True)
                return last

            def last_products(i, kinds):
                scatter(i, 0, kinds)
                pe.wait_ge(acc_added[SETS - 2], i)
                pe.wait_ge(wcat_ready, 1)
                for n in range(len(RUNS) - 1):
                    project(n).then_inc(projected, 1)
                scatter_late(i - 1)
                for j in range(1, len(kinds)):
                    scatter(i, j, kinds)

            def sum_reach():
                pe.wait_ge(reach_ready, 4)
                pe.wait_ge(wcat_ready, 1)
                nc.tensor.matmul(small[0:1, 1, 0:1], reach[:, 3:4], ones[:, :], start=True,
                                 stop=True).then_inc(reach_summed, 1)

            flag = []

            def read_flag():
                pe.wait_ge(flag_ready, 1)
                flag.append(pe.value_load(outside[0:1, 0:1], min_val=0, max_val=P))

            rounds(pe, products, after_first=sum_reach, before_last=read_flag, last_body=last_products)

            pe.wait_ge(acc_added[0], FULL + 1)
            with pe.If(flag[0] > 0):
                def scatter_again(s, start):
                    pe.wait_ge(gen_attr, (s + 1) * (16 * HALVES))
                    pe.wait_ge(gen_rows, (s + 1) * (16 * TILES))
                    for b in range(BLOCKS):
                        width = min(BANK, N - b * BANK)
                        pe.wait_ge(gen_S, s * BLOCKS + (b + 1))
                        pe.wait_ge(gen_added, s * BLOCKS + (b + 1))
                        for t in range(TILES):
                            last = nc.tensor.matmul(acc[0][0:G, 0:width], V[:, 1, t, :], S_gen[:, t, 0:width],
                                                    start=(t == 0), stop=(t == TILES - 1))
                        last.then_inc(gen_acc, 1)

                superchunks(pe, scatter_again)
                pe.wait_ge(gen_added, NS * BLOCKS + 1)
                for n in range(len(RUNS) - 1):
                    last = project(n)
                last.then_inc(gen_projected, 1)

            project(len(RUNS) - 1).then_inc(projected, 1)


def build(nc, *args):
    gnn_kernel(nc, *args)

_INS = ['x','src','dst','edge_attr_64','edge_weight1','L0_gnn_W_node','L0_gnn_W_review']
_OUTS = [((3125, 16), 'float32')]

def kernel(**inputs):
    import numpy as _np
    import concourse.bacc as _bacc
    from concourse import mybir as _mybir
    from concourse.bass_utils import run_bass_kernel_spmd as _run

    nc = _bacc.Bacc("TRN2", target_bir_lowering=False, num_devices=1)
    arrays, args = {}, []
    for name in _INS:
        a = _np.ascontiguousarray(inputs[name])
        arrays[f"in_{name}_dram"] = a
        args.append(nc.dram_tensor(f"in_{name}_dram", a.shape, _mybir.dt.from_np(a.dtype), kind="ExternalInput").ap())
    for i, (shape, dtype) in enumerate(_OUTS):
        dt = _mybir.dt.from_np(_np.dtype(dtype))
        args.append(nc.dram_tensor(f"out_{i}_dram", shape, dt, kind="ExternalOutput").ap())
    build(nc, *args)
    r = _run(nc, [arrays], core_ids=[0])
    got = tuple(r.results[0][f"out_{i}_dram"] for i in range(len(_OUTS)))
    return got[0]
```
